# Optimizing a Trainium2 kernel written in Bass

```python
import numpy as np
import jax
import jax.numpy as jnp

def _softmax(x, axis=-1):
    return jax.nn.softmax(x, axis=axis)

def _gelu(x):
    return jax.nn.gelu(x, approximate=True)

def _silu(x):
    return jax.nn.silu(x)

def _sigmoid(x):
    return jax.nn.sigmoid(x)

def _layernorm(x, axis=-1, eps=1e-05):
    m = jnp.mean(x, axis=axis, keepdims=True)
    v = jnp.var(x, axis=axis, keepdims=True)
    return (x - m) / jnp.sqrt(v + eps)

def _scatter_add(tgt, idx, src, axis=0):
    return tgt.at[idx].add(src)

def _segment_sum(src, seg, n):
    return jax.ops.segment_sum(src, seg, n)
kernel_name = 'mk_lm_tower_d1_tok_ids1024_r4_67f6c7'

def setup_inputs(seed: int=0):
    np.random.seed(seed)
    _w = jnp.asarray

    def _rec_inputs():
        import jax
        import jax.numpy as jnp
        _rk = jax.random.key(seed)
        x = jax.random.randint(jax.random.fold_in(_rk, 1), (64, 128), 0, 12564, jnp.int32)
        return x
    x = _rec_inputs()

    def _L0_tok_setup():
        import jax, jax.numpy as jnp
        import numpy as np
        VOCAB, DIM, N_DOM, EXP = (50257, 256, 8, 32)
        B, S = (4, 1024)
        key = jax.random.key(seed)
        k1, k2, k3, k4, k5, k6 = jax.random.split(key, 6)
        token_ids = jax.random.randint(k1, (B, S), 0, VOCAB, dtype=jnp.int32)
        dom = jax.random.randint(k2, (VOCAB,), 0, N_DOM, dtype=jnp.int32)
        routed = jax.random.uniform(k3, (VOCAB,)) < 0.2
        domain_map = jnp.where(routed, dom, jnp.int32(-1))
        emb_table = jax.random.normal(k4, (VOCAB, DIM), dtype=jnp.float32) * 0.02
        lim_e = 0.1 * np.sqrt(6.0 / (DIM + EXP))
        lim_p = 0.1 * np.sqrt(6.0 / (EXP + DIM))
        W_exp = jax.random.uniform(k5, (N_DOM, EXP, DIM), minval=-lim_e, maxval=lim_e, dtype=jnp.float32)
        W_proj = jax.random.uniform(k6, (N_DOM, DIM, EXP), minval=-lim_p, maxval=lim_p, dtype=jnp.float32)
        return {'token_ids': token_ids, 'domain_map': domain_map, 'emb_table': emb_table, 'W_exp': W_exp, 'W_proj': W_proj}
    _L0_tok_all = _L0_tok_setup()
    _L0_tok_in = {k: v for k, v in _L0_tok_all.items() if k in ('domain_map', 'emb_table', 'W_exp', 'W_proj')}
    del _L0_tok_all

    def _L0_attn_setup():
        import jax, jax.numpy as jnp
        import numpy as np
        import math
        D_MODEL = 256
        N_HEADS = 16
        D_HEAD = D_MODEL // N_HEADS
        WINDOW_LEN = 128
        DILATION = 4
        SEQ = 768
        BATCH = 1

        def _causal_windowed_bias(seq_len):
            idx = jnp.arange(seq_len)
            diff = idx[:, None] - idx[None, :]
            allowed = (diff >= 0) & (diff // DILATION < WINDOW_LEN) & (diff % DILATION == 0)
            return jnp.where(allowed, 0.0, -jnp.inf).astype(jnp.float32)
        key = jax.random.key(seed)
        ks = jax.random.split(key, 10)

        def xavier(k, shape):
            fan_out, fan_in = shape
            lim = math.sqrt(6.0 / (fan_in + fan_out))
            return jax.random.uniform(k, shape, jnp.float32, -lim, lim)
        return {'x': jax.random.normal(ks[0], (SEQ, BATCH, D_MODEL), jnp.float32), 'beta': 0.1 * jax.random.normal(ks[1], (N_HEADS,), jnp.float32), 'Wq': xavier(ks[2], (D_MODEL, D_MODEL)), 'bq': jnp.zeros((D_MODEL,), jnp.float32), 'Wk': xavier(ks[3], (D_MODEL, D_MODEL)), 'bk': jnp.zeros((D_MODEL,), jnp.float32), 'Wv': xavier(ks[4], (D_MODEL, D_MODEL)), 'bv': jnp.zeros((D_MODEL,), jnp.float32), 'Wo': xavier(ks[5], (D_MODEL, D_MODEL)), 'bo': jnp.zeros((D_MODEL,), jnp.float32)}
    _L0_attn_all = _L0_attn_setup()
    _L0_attn_in = {k: v for k, v in _L0_attn_all.items() if k in ('beta', 'Wq', 'bq', 'Wk', 'bk', 'Wv', 'bv', 'Wo', 'bo')}
    del _L0_attn_all

    def _L0_ffn_setup():
        import jax, jax.numpy as jnp
        import numpy as np
        B, S, H, E = (8, 1024, 256, 8)
        key = jax.random.key(seed)
        k1, k2, k3 = jax.random.split(key, 3)
        x = jax.random.normal(k1, (B, S, H), dtype=jnp.float32)
        Wg = jax.random.normal(k2, (H, E), dtype=jnp.float32) * (1.0 / np.sqrt(H))
        bg = jnp.zeros((E,), dtype=jnp.float32)
        We = jax.random.normal(k3, (H, H), dtype=jnp.float32) * (1.0 / np.sqrt(H))
        be = jnp.zeros((H,), dtype=jnp.float32)
        return {'x': x, 'Wg': Wg, 'bg': bg, 'We': We, 'be': be}
    _L0_ffn_all = _L0_ffn_setup()
    _L0_ffn_in = {k: v for k, v in _L0_ffn_all.items() if k in ('Wg', 'bg', 'We', 'be')}
    del _L0_ffn_all
    return {'x': x, 'L0_tok_domain_map': _L0_tok_in['domain_map'], 'L0_tok_emb_table': _L0_tok_in['emb_table'], 'L0_tok_W_exp': _L0_tok_in['W_exp'], 'L0_tok_W_proj': _L0_tok_in['W_proj'], 'L0_attn_beta': _L0_attn_in['beta'], 'L0_attn_Wq': _L0_attn_in['Wq'], 'L0_attn_bq': _L0_attn_in['bq'], 'L0_attn_Wk': _L0_attn_in['Wk'], 'L0_attn_bk': _L0_attn_in['bk'], 'L0_attn_Wv': _L0_attn_in['Wv'], 'L0_attn_bv': _L0_attn_in['bv'], 'L0_attn_Wo': _L0_attn_in['Wo'], 'L0_attn_bo': _L0_attn_in['bo'], 'L0_ffn_Wg': _L0_ffn_in['Wg'], 'L0_ffn_bg': _L0_ffn_in['bg'], 'L0_ffn_We': _L0_ffn_in['We'], 'L0_ffn_be': _L0_ffn_in['be']}

def reference(x, L0_tok_domain_map, L0_tok_emb_table, L0_tok_W_exp, L0_tok_W_proj, L0_attn_beta, L0_attn_Wq, L0_attn_bq, L0_attn_Wk, L0_attn_bk, L0_attn_Wv, L0_attn_bv, L0_attn_Wo, L0_attn_bo, L0_ffn_Wg, L0_ffn_bg, L0_ffn_We, L0_ffn_be):
    import jax
    import jax.numpy as jnp

    def _L0_tok_ref(token_ids, domain_map, emb_table, W_exp, W_proj):
        import jax, jax.numpy as jnp
        import numpy as np
        VOCAB, DIM, N_DOM, EXP = (50257, 256, 8, 32)
        B, S = (4, 1024)
        base = emb_table[token_ids]
        dom = domain_map[token_ids]
        out = base
        n_domains = W_exp.shape[0]
        for d in range(n_domains):
            mask = (dom == d)[..., None].astype(base.dtype)
            expanded = jnp.einsum('bsd,ed->bse', base, W_exp[d])
            corr = jnp.einsum('bse,de->bsd', expanded, W_proj[d])
            out = out + 0.1 * corr * mask
        return out

    def _L0_attn_ref(x, beta, Wq, bq, Wk, bk, Wv, bv, Wo, bo):
        import jax, jax.numpy as jnp
        import numpy as np
        import math
        D_MODEL = 256
        N_HEADS = 16
        D_HEAD = D_MODEL // N_HEADS
        WINDOW_LEN = 128
        DILATION = 4
        SEQ = 768
        BATCH = 1

        def _causal_windowed_bias(seq_len):
            idx = jnp.arange(seq_len)
            diff = idx[:, None] - idx[None, :]
            allowed = (diff >= 0) & (diff // DILATION < WINDOW_LEN) & (diff % DILATION == 0)
            return jnp.where(allowed, 0.0, -jnp.inf).astype(jnp.float32)
        s, b, d = x.shape

        def split_heads(t):
            return t.reshape(s, b, N_HEADS, D_HEAD).transpose(1, 2, 0, 3)
        q = split_heads(x @ Wq.T + bq)
        k = split_heads(x @ Wk.T + bk)
        v = split_heads(x @ Wv.T + bv)
        q = q / (math.sqrt(D_HEAD) * jnp.exp(beta)[None, :, None, None])
        bias = _causal_windowed_bias(s)
        scores = jnp.einsum('bhsd,bhtd->bhst', q, k) + bias
        attn = jax.nn.softmax(scores, axis=-1)
        ctx = jnp.einsum('bhst,bhtd->bhsd', attn, v)
        ctx = ctx.transpose(2, 0, 1, 3).reshape(s, b, d)
        return ctx @ Wo.T + bo

    def _L0_ffn_ref(x, Wg, bg, We, be):
        import jax, jax.numpy as jnp
        import numpy as np
        B, S, H, E = (8, 1024, 256, 8)
        b, s, h = x.shape
        tokens = x.reshape(-1, h)
        logits = tokens @ Wg + bg
        probs = jax.nn.softmax(logits, axis=1)
        best = jnp.argmax(logits, axis=1)
        best_p = jnp.take_along_axis(probs, best[:, None], axis=1)[:, 0]
        expert_out = tokens @ We + be
        out = expert_out * best_p[:, None]
        return out.reshape(b, s, h)
    h = _L0_tok_ref(x, L0_tok_domain_map, L0_tok_emb_table, L0_tok_W_exp, L0_tok_W_proj)
    h = h + _L0_attn_ref(_layernorm(h, axis=-1), L0_attn_beta, L0_attn_Wq, L0_attn_bq, L0_attn_Wk, L0_attn_bk, L0_attn_Wv, L0_attn_bv, L0_attn_Wo, L0_attn_bo)
    h = h + _L0_ffn_ref(_layernorm(h, axis=-1), L0_ffn_Wg, L0_ffn_bg, L0_ffn_We, L0_ffn_be)
    return h

_drawn_inputs = setup_inputs


def setup_inputs(seed=0):
    import zlib

    import numpy as np

    out = dict(_drawn_inputs(seed))
    spreads = {'L0_attn_bq': (0.0, 0.1),
     'L0_attn_bk': (0.0, 0.8),
     'L0_attn_bv': (0.0, 0.1),
     'L0_attn_bo': (0.0, 0.1),
     'L0_ffn_bg': (0.0, 0.369),
     'L0_ffn_be': (0.0, 0.1)}
    factors = {'L0_tok_W_exp': 8.0, 'L0_tok_W_proj': 8.0}
    for name, (base, spread) in spreads.items():
        noise = np.random.default_rng([zlib.crc32(name.encode()), seed]).standard_normal(out[name].shape)
        drawn = base * np.exp(spread * noise) if base else spread * noise
        out[name] = jnp.asarray(drawn.astype(out[name].dtype))
    for name, factor in factors.items():
        out[name] = (out[name] * factor).astype(out[name].dtype)
    return out
```

```python
import concourse.bass as bass
from concourse import mybir
from contextlib import ExitStack

FP32 = mybir.dt.float32
BF16 = mybir.dt.bfloat16
INT32 = mybir.dt.int32
ALU = mybir.AluOpType
ACT = mybir.ActivationFunctionType
AX = mybir.AxisListType

SEQ, BATCH = 64, 128
DIM = 256
VOCAB = 50257
N_DOM, EXPAND = 8, 32
HEADS, D_HEAD = 16, 16
DILATION = 4
N_EXP = 8
LN_EPS = 1e-5

TOKENS = SEQ * BATCH
TILE = 128
CHUNK = 2 * TILE
N_CHUNK = TOKENS // CHUNK
BLOCK = 32
BLOCKS = TILE // BLOCK
HALVES = DIM // 128
QUAD_HEADS = HEADS // 4

C_IDENT, C_MASK, C_SLOT, C_DOMAIN, C_END = 0, 128, 160, 164, 166


class Chunk:

    def __init__(self, offset, j=None):
        self.par = offset % 2
        self.k = offset if j is None else 2 * j + offset
        self.pair = offset // 2 if j is None else j + offset // 2


LEAD_IN, ENTER, QKV, CTX, FFN, OUT = 1, 0, -1, -2, -3, -4
LOOP_FROM, LOOP_TO = 6, 30
FIRST_STEP, LAST_STEP = -1, N_CHUNK - 1 - OUT


def run_steps(engine, step):

    def peeled(n):
        step(lambda lag: Chunk(n + lag) if 0 <= n + lag < N_CHUNK else None)

    for n in range(FIRST_STEP, LOOP_FROM):
        peeled(n)
    with engine.Fori(0, (LOOP_TO - LOOP_FROM) // 2) as j:
        for s in range(2):
            step(lambda lag: Chunk(LOOP_FROM + s + lag, j))
    for n in range(LOOP_TO, LAST_STEP + 1):
        peeled(n)


def wait_past(engine, sem, count):
    if not isinstance(count, int) or count > 0:
        engine.wait_ge(sem, count)


def at_most_all(count):
    return min(count, N_CHUNK) if isinstance(count, int) else count


def build_lm_tower(nc, ids, domain_map, emb_table, w_exp, w_proj, wq, wk, wv, wo, bo, wg, bg, we, be,
                   columns, consts, out):
    ctx = ExitStack()
    with ctx:
        def sb(name, shape, dt=FP32):
            return ctx.enter_context(nc.sbuf_tensor(name, shape, dt))

        def sem(name):
            return ctx.enter_context(nc.semaphore(name))

        const_sb = sb("const_sb", [128, C_END])
        ident = const_sb[:, C_IDENT:C_IDENT + 128]
        causal = const_sb[:, C_MASK:C_MASK + BLOCK]
        slot_mask = const_sb[:, C_SLOT:C_SLOT + 4]
        row_domain = const_sb[:, C_DOMAIN:C_DOMAIN + 2]
        ident_bf = sb("ident_bf", [128, 128], BF16)
        ones_bf = sb("ones_bf", [128, 128], BF16)
        w_exp_sb = sb("w_exp_sb", [128, HALVES, DIM])
        w_proj_sb = sb("w_proj_sb", [128, HALVES, DIM])
        wq_sb = sb("wq_sb", [128, HALVES, DIM])
        wk_sb = sb("wk_sb", [128, HALVES, DIM])
        wv_sb = sb("wv_sb", [128, HALVES, DIM])
        wo_sb = sb("wo_sb", [128, HALVES, DIM])
        wf_sb = sb("wf_sb", [128, HALVES, DIM + N_EXP])
        columns_sb = sb("columns_sb", [128, 4, HALVES])
        bq_sb, bk_sb, bv_sb, beta_sb = (columns_sb[:, n, :] for n in range(4))
        q_scale = sb("q_scale", [128, HALVES])
        q_bias = sb("q_bias", [128, HALVES])
        N_BIAS = 2 * DIM + N_EXP
        bias_row = sb("bias_row", [1, N_BIAS])
        bias_rest = sb("bias_rest", [1, N_BIAS])
        bias_rest2 = sb("bias_rest2", [1, N_BIAS])
        bias_parts = sb("bias_parts", [128, N_BIAS], BF16)
        minus_half = sb("minus_half", [128, 2])
        minus_one = sb("minus_one", [128, 2])
        eps = sb("eps", [128, 2])

        def pair(name, shape, dt=FP32):
            return [sb(f"{name}{p}", shape, dt) for p in range(2)]

        id_sb = pair("id_sb", [128, 2], INT32)
        dom_int = pair("dom_int", [128, 2], INT32)
        dom_bf = pair("dom_bf", [128, 2], BF16)
        base = pair("base", [128, 2, DIM])
        base_t = pair("base_t", [128, HALVES, CHUNK])
        dom_row = pair("dom_row", [128, CHUNK])
        expert_t = pair("expert_t", [128, HALVES, CHUNK])
        h1 = pair("h1", [128, 2, DIM])
        xn1 = pair("xn1", [128, 2, DIM])
        xn1_t = pair("xn1_t", [128, HALVES, CHUNK])
        q_t = pair("q_t", [128, HALVES, 2, CHUNK])
        k_t = pair("k_t", [128, HALVES, CHUNK])
        k_slots = pair("k_slots", [128, HALVES, 4, CHUNK])
        v_sb = pair("v_sb", [128, 2, DIM])
        v_diag = pair("v_diag", [128, 2, BLOCKS, DIM])
        scores = pair("scores", [128, 16, BLOCK])
        shifted = pair("shifted", [128, 16, BLOCK])
        probs = pair("probs", [128, 16, BLOCK])
        probs_n = pair("probs_n", [128, 16, BLOCK])
        probs_t = [[sb(f"probs_t{p}{t}", [128, 16, BLOCK]) for t in range(2)] for p in range(2)]
        score_max = pair("score_max", [128, 16])
        prob_sum = pair("prob_sum", [128, 16])
        prob_inv = pair("prob_inv", [128, 16])
        ctx_t = pair("ctx_t", [128, HALVES, CHUNK])
        h2 = pair("h2", [128, 2, DIM])
        xn2 = pair("xn2", [128, 2, DIM])
        xn2_t = pair("xn2_t", [128, HALVES, CHUNK])
        out_sb = pair("out_sb", [128, 2, DIM])
        gate_max = pair("gate_max", [128, 2])
        gate_shift = pair("gate_shift", [128, 2, N_EXP])
        gate_exp = pair("gate_exp", [128, 2, N_EXP])
        gate_sum = pair("gate_sum", [128, 2])
        gate_best = pair("gate_best", [128, 2])
        ln = []
        for w in (1, 2):
            ln.append(dict(
                raw=pair(f"ln{w}_raw", [128, 2, 6]), stat=pair(f"ln{w}_stat", [128, 2, 2]),
                var=pair(f"ln{w}_var", [128, 2]), rstd=pair(f"ln{w}_rstd", [128, 2]),
                mr=pair(f"ln{w}_mr", [128, 2]), shift=pair(f"ln{w}_shift", [128, 2])))

        ps = ctx.enter_context(nc.psum_tensor("ps", [128, 8, 512], FP32))

        def halves(bank):
            return ps[:, bank, :].rearrange("p (a n) -> p a n", a=2)

        ps_xn1_t, ps_attn = halves(0), halves(0)
        ps_expert, ps_xn2_t = halves(1), halves(1)
        ps_q, ps_k = halves(2), halves(3)
        ps_scores = [ps[:, 2 + t, :].rearrange("p (m t) -> p m t", t=BLOCK) for t in range(2)]
        ps_ctx, ps_base_t = halves(4), halves(4)
        ps_ffn = ps[:, 5:7, 0:DIM + N_EXP]
        ps_tok = halves(6)
        ps_v = halves(7)
        ps_dom = ps[:, 7, 0:CHUNK]

        s_consts, s_wexp, s_wproj, s_qkvw, s_wof, s_rows, s_columns = (
            sem(n) for n in ("consts_in", "wexp_in", "wproj_in", "qkv_weights_in", "wo_wffn_in", "bias_rows_in",
                             "columns_in"))
        s_passed = sem("passed")
        s_setup_v, s_setup_g, s_setup_a, s_setup_p = (sem(n) for n in ("setup_vector", "setup_pool", "setup_act",
                                                                       "setup_pe"))
        ids_in = [sem(f"ids_in{p}") for p in range(2)]
        base_in = [sem(f"base_in{p}") for p in range(2)]
        dom_in = [sem(f"dom_in{p}") for p in range(2)]
        v_moved = [sem(f"v_moved{p}") for p in range(2)]
        out_stored = [sem(f"out_stored{p}") for p in range(2)]
        dom_cast = sem("dom_cast")
        base_turned, dom_spread, expert_done, tok_done, xn1_turned = (
            sem(n) for n in ("base_turned", "dom_spread", "expert_done", "tok_done", "xn1_turned"))
        q_done, k_done, v_done, scores_done, ctx_done, attn_done, xn2_turned, ffn_done = (
            sem(n) for n in ("q_done", "k_done", "v_done", "scores_done", "ctx_done", "attn_done", "xn2_turned",
                             "ffn_done"))
        base_t_saved, dom_saved, xn1_saved, xn1_t_saved, k_saved, v_saved, exp_done, ctx_saved, xn2_saved, \
            xn2_t_saved, gate_exp_done = (
                sem(n) for n in ("base_t_saved", "dom_saved", "xn1_saved", "xn1_t_saved", "k_saved", "v_saved",
                                 "exp_done", "ctx_saved", "xn2_saved", "xn2_t_saved", "gate_exp_done"))
        expert_masked, h1_saved, q_saved, k_spread, scores_masked, max_done, sum_done, inv_done, probs_turned, \
            h2_saved, gate_max_done, gate_shifted, gate_sum_done, gate_ready, out_saved = (
                sem(n) for n in ("expert_masked", "h1_saved", "q_saved", "k_spread", "scores_masked", "max_done",
                                 "sum_done", "inv_done", "probs_turned", "h2_saved", "gate_max_done",
                                 "gate_shifted", "gate_sum_done", "gate_ready", "out_saved"))
        ln_raw = [sem(f"ln{w}_raw_done") for w in (1, 2)]
        ln_stat = [sem(f"ln{w}_stat_done") for w in (1, 2)]
        scores_shifted, probs_scaled = sem("scores_shifted"), sem("probs_scaled")
        ln_var = [sem(f"ln{w}_var_done") for w in (1, 2)]
        ln_rstd = [sem(f"ln{w}_rstd_done") for w in (1, 2)]
        ln_mr = [sem(f"ln{w}_mr_done") for w in (1, 2)]
        ln_shift = [sem(f"ln{w}_shift_done") for w in (1, 2)]

        def stand_alone(engine, c):
            if not isinstance(c.k, int):
                engine.sem_inc(s_passed, 1)

        ids_by_chunk = ids.rearrange("(c p) t -> c p t", p=128)
        out_by_chunk = out.rearrange("(c t p) f -> c p t f", t=2, p=128)
        block = ctx.enter_context(nc.Block())

        @block.sync
        def _(sp):
            def load_ids(c):
                wait_past(sp, base_in[c.par], 32 * c.pair)
                wait_past(sp, dom_in[c.par], 32 * c.pair)
                stand_alone(sp, c)
                sp.dma_start(id_sb[c.par][:, :], ids_by_chunk[c.k]).then_inc(ids_in[c.par], 16)

            load_ids(Chunk(0))
            load_ids(Chunk(1))
            sp.dma_start(const_sb[:, :], consts).then_inc(s_consts, 16)
            sp.dma_start(columns_sb[:, :, :], columns).then_inc(s_columns, 16)
            sp.dma_start(w_exp_sb[:, :, :], w_exp.rearrange("(a p) m -> p a m", p=128)).then_inc(s_wexp, 16)
            sp.dma_start(w_proj_sb[:, :, :], w_proj.rearrange("(a p) m -> p a m", p=128)).then_inc(s_wproj, 16)
            for w, dst in ((wq, wq_sb), (wk, wk_sb), (wv, wv_sb)):
                sp.dma_start(dst[:, :, :], w.rearrange("(a p) m -> p a m", p=128)).then_inc(s_qkvw, 16)
            sp.dma_start(wo_sb[:, :, :], wo.rearrange("(a p) m -> p a m", p=128)).then_inc(s_wof, 16)
            sp.dma_start(wf_sb[:, :, 0:DIM], we.rearrange("(a p) m -> p a m", p=128)).then_inc(s_wof, 16)
            sp.dma_start(wf_sb[:, :, DIM:], wg.rearrange("(a p) m -> p a m", p=128)).then_inc(s_wof, 16)
            for b, at, n in ((bo, 0, DIM), (be, DIM, DIM), (bg, 2 * DIM, N_EXP)):
                sp.dma_start(bias_row[0:1, at:at + n], b.rearrange("(a n) -> a n", a=1)).then_inc(s_rows, 16)

            def move_v(c):
                sp.wait_ge(v_saved, c.k + 1)
                stand_alone(sp, c)
                wait_past(sp, ctx_done, c.k - 1)
                if isinstance(c.k, int) and c.k < 2:
                    sp.wait_ge(s_setup_g, 7)
                stand_alone(sp, c)
                for b in range(BLOCKS):
                    for u in range(4):
                        sp.dma_start(v_diag[c.par][32 * u:32 * u + 32, :, b, 64 * u:64 * u + 64],
                                     v_sb[c.par][32 * b:32 * b + 32, :, 64 * u:64 * u + 64])\
                          .then_inc(v_moved[c.par], 16)

            def step(chunk_of):
                if (c := chunk_of(ENTER + 2)) is not None:
                    if not (isinstance(c.k, int) and c.k < 2):
                        load_ids(c)
                if (c := chunk_of(QKV)) is not None:
                    move_v(c)
                if (c := chunk_of(OUT)) is not None:
                    sp.wait_ge(out_saved, 2 * c.k + 2)
                    stand_alone(sp, c)
                    sp.dma_start(out_by_chunk[c.k], out_sb[c.par][:, :, :]).then_inc(out_stored[c.par], 16)

            run_steps(sp, step)
            for p in range(2):
                sp.wait_ge(out_stored[p], 16 * (N_CHUNK // 2))

        @block.gpsimd
        def _(pool):
            def gather(c):
                pool.wait_ge(ids_in[c.par], 16 * c.pair + 16)
                wait_past(pool, h1_saved, c.k - 1)
                wait_past(pool, dom_cast, c.k - 1)
                stand_alone(pool, c)
                for t in range(2):
                    pool.indirect_dma_start(base[c.par][:, t, :], None, emb_table,
                                            bass.IndirectOffsetOnAxis(id_sb[c.par][:, t:t + 1], 0))\
                        .then_inc(base_in[c.par], 16)
                    pool.indirect_dma_start(dom_int[c.par][:, t:t + 1], None, domain_map,
                                            bass.IndirectOffsetOnAxis(id_sb[c.par][:, t:t + 1], 0))\
                        .then_inc(dom_in[c.par], 16)

            def cast_domains(c):
                pool.wait_ge(dom_in[c.par], 32 * c.pair + 32)
                wait_past(pool, dom_spread, c.k - 1)
                stand_alone(pool, c)
                pool.tensor_copy(dom_bf[c.par][:, :], dom_int[c.par][:, :]).then_inc(dom_cast, 1)

            def layernorm_scalars(w, c):
                L, p = ln[w], c.par
                pool.wait_ge(ln_stat[w], c.k + 1)
                wait_past(pool, xn1_saved if w == 0 else xn2_saved, c.k - 1)
                pool.tensor_tensor(L["var"][p][:, :], L["stat"][p][:, :, 1], eps[:, :], ALU.add)\
                    .then_inc(ln_var[w], 1)
                pool.wait_ge(ln_var[w], c.k + 1)
                pool.tensor_tensor(L["rstd"][p][:, :], L["var"][p][:, :], minus_half[:, :], ALU.pow)\
                    .then_inc(ln_rstd[w], 1)
                pool.wait_ge(ln_rstd[w], c.k + 1)
                pool.tensor_tensor(L["mr"][p][:, :], L["stat"][p][:, :, 0], L["rstd"][p][:, :], ALU.mult)\
                    .then_inc(ln_mr[w], 1)
                pool.wait_ge(ln_mr[w], c.k + 1)
                pool.tensor_tensor(L["shift"][p][:, :], L["mr"][p][:, :], minus_one[:, :], ALU.mult)\
                    .then_inc(ln_shift[w], 1)

            def shift_scores(c, t):
                pool.wait_ge(max_done, 2 * c.k + t + 1)
                wait_past(pool, exp_done, 2 * c.k + t - 1)
                pool.tensor_tensor(shifted[t][:, :, :], scores[t][:, :, :],
                                   score_max[t][:, :].unsqueeze(2).to_broadcast([128, 16, BLOCK]),
                                   ALU.subtract).then_inc(scores_shifted, 1)

            def scale_probs(c, t):
                pool.wait_ge(inv_done, 2 * c.k + t + 1)
                wait_past(pool, probs_turned, 2 * c.k + t - 1)
                pool.tensor_tensor(probs_n[t][:, :, :], probs[t][:, :, :],
                                   prob_inv[t][:, :].unsqueeze(2).to_broadcast([128, 16, BLOCK]),
                                   ALU.mult).then_inc(probs_scaled, 1)

            gather(Chunk(0))
            gather(Chunk(1))
            for tile, value in ((minus_half, -0.5), (minus_one, -1.0), (eps, LN_EPS)):
                pool.memset(tile[:, :], value).then_inc(s_setup_g, 1)
            for p in range(2):
                pool.memset(q_t[p][:, :, :, :], 0.0).then_inc(s_setup_g, 1)
            for p in range(2):
                pool.memset(v_diag[p][:, :, :, :], 0.0).then_inc(s_setup_g, 1)
            pool.wait_ge(s_setup_g, 7)

            def step(chunk_of):
                if (c := chunk_of(CTX)) is not None:
                    scale_probs(c, 0)
                    scale_probs(c, 1)
                if (c := chunk_of(ENTER + 2)) is not None:
                    if not (isinstance(c.k, int) and c.k < 2):
                        gather(c)
                if (c := chunk_of(CTX)) is not None:
                    layernorm_scalars(1, c)
                if (c := chunk_of(ENTER)) is not None:
                    layernorm_scalars(0, c)
                if (c := chunk_of(LEAD_IN)) is not None:
                    cast_domains(c)
                if (c := chunk_of(QKV)) is not None:
                    shift_scores(c, 0)
                    shift_scores(c, 1)

            run_steps(pool, step)

        @block.scalar
        def _(act):
            act.wait_ge(s_columns, 16)
            act.activation(q_scale[:, :], beta_sb[:, :], ACT.Exp, scale=-1.0).then_inc(s_setup_a, 1)

            def save_base_t(c):
                act.wait_ge(base_turned, c.k + 1)
                wait_past(act, expert_done, c.k - 1)
                act.activation(base_t[c.par][:, :, :], ps_base_t, ACT.Copy).then_inc(base_t_saved, 1)
                act.wait_ge(dom_spread, c.k + 1)
                wait_past(act, expert_masked, c.k - 1)
                act.activation(dom_row[c.par][:, :], ps_dom, ACT.Copy).then_inc(dom_saved, 1)

            def normalise(w, c, src, dst, saved, turned):
                L, p = ln[w], c.par
                act.wait_ge(ln_shift[w], c.k + 1)
                wait_past(act, turned, c.k - 1)
                for t in range(2):
                    last = act.activation(dst[p][:, t, :], src[p][:, t, :], ACT.Identity,
                                          scale=L["rstd"][p][:, t:t + 1], bias=L["shift"][p][:, t:t + 1])
                last.then_inc(saved, 1)

            def save_k(c):
                act.wait_ge(k_done, c.k + 1)
                wait_past(act, k_spread, c.k - 1)
                for a in range(HALVES):
                    last = act.activation(k_t[c.par][:, a, :], ps_k[:, a, :], ACT.Identity,
                                          bias=bk_sb[:, a:a + 1])
                last.then_inc(k_saved, 1)

            def exponentials(c, t):
                act.wait_ge(scores_shifted, 2 * c.k + t + 1)
                wait_past(act, probs_scaled, 2 * c.k + t - 1)
                act.activation(probs[t][:, :, :], shifted[t][:, :, :], ACT.Exp).then_inc(exp_done, 1)

            def step(chunk_of):
                if (c := chunk_of(QKV)) is not None:
                    act.wait_ge(xn1_turned, c.k + 1)
                    wait_past(act, v_done, c.k - 1)
                    act.activation(xn1_t[c.par][:, :, :], ps_xn1_t, ACT.Copy).then_inc(xn1_t_saved, 1)
                if (c := chunk_of(OUT)) is not None:
                    act.wait_ge(gate_shifted, c.k + 1)
                    wait_past(act, gate_sum_done, c.k - 1)
                    act.activation(gate_exp[c.par][:, :, :], gate_shift[c.par][:, :, :], ACT.Exp)\
                       .then_inc(gate_exp_done, 1)
                if (c := chunk_of(QKV)) is not None:
                    save_k(c)
                if (c := chunk_of(CTX)) is not None:
                    act.wait_ge(ctx_done, c.k + 1)
                    wait_past(act, attn_done, c.k - 1)
                    act.activation(ctx_t[c.par][:, :, :], ps_ctx, ACT.Copy).then_inc(ctx_saved, 1)
                if (c := chunk_of(QKV)) is not None:
                    act.wait_ge(v_done, c.k + 1)
                    wait_past(act, v_moved[c.par], 256 * c.pair)
                    act.activation(v_sb[c.par][:, :, :], ps_v, ACT.Copy).then_inc(v_saved, 1)
                if (c := chunk_of(CTX)) is not None:
                    normalise(1, c, h2, xn2, xn2_saved, xn2_turned)
                if (c := chunk_of(FFN)) is not None:
                    act.wait_ge(xn2_turned, c.k + 1)
                    wait_past(act, ffn_done, c.k - 1)
                    act.activation(xn2_t[c.par][:, :, :], ps_xn2_t, ACT.Copy).then_inc(xn2_t_saved, 1)
                if (c := chunk_of(ENTER)) is not None:
                    normalise(0, c, h1, xn1, xn1_saved, xn1_turned)
                if (c := chunk_of(LEAD_IN)) is not None:
                    save_base_t(c)
                if (c := chunk_of(QKV)) is not None:
                    exponentials(c, 0)
                    exponentials(c, 1)

            run_steps(act, step)

        @block.vector
        def _(dve):
            dve.wait_ge(s_consts, 16)
            dve.tensor_copy(ident_bf[:, :], ident)
            dve.memset(ones_bf[:, :], 1.0)
            dve.memset(bias_parts[:, :], 0.0).then_inc(s_setup_v, 1)
            dve.wait_ge(s_setup_a, 1)
            dve.tensor_scalar(q_scale[:, :], q_scale[:, :], float(D_HEAD) ** -0.5, None, ALU.mult)\
               .then_inc(s_setup_v, 1)
            dve.wait_ge(s_setup_v, 2)
            dve.tensor_tensor(q_bias[:, :], bq_sb[:, :], q_scale[:, :], ALU.mult).then_inc(s_setup_v, 1)
            dve.wait_ge(s_setup_v, 3)

            def split_biases():
                dve.wait_ge(s_setup_p, 1)
                dve.wait_ge(s_rows, 16 * 3)
                dve.tensor_tensor(bias_row[0:1, 0:DIM], ps[0:1, 5, 0:DIM], bias_row[0:1, 0:DIM], ALU.add)\
                   .then_inc(s_setup_v, 1)
                dve.wait_ge(s_setup_v, 4)
                dve.tensor_copy(bias_parts[0:1, :], bias_row[0:1, :]).then_inc(s_setup_v, 1)
                dve.wait_ge(s_setup_v, 5)
                dve.tensor_tensor(bias_rest[0:1, :], bias_row[0:1, :], bias_parts[0:1, :], ALU.subtract)\
                   .then_inc(s_setup_v, 1)
                dve.wait_ge(s_setup_v, 6)
                dve.tensor_copy(bias_parts[32:33, :], bias_rest[0:1, :])
                dve.tensor_copy(bias_row[0:1, :].bitcast(BF16)[:, 0:N_BIAS], bias_rest[0:1, :])\
                   .then_inc(s_setup_v, 1)
                dve.wait_ge(s_setup_v, 7)
                dve.tensor_tensor(bias_rest2[0:1, :], bias_rest[0:1, :],
                                  bias_row[0:1, :].bitcast(BF16)[:, 0:N_BIAS], ALU.subtract)\
                   .then_inc(s_setup_v, 1)
                dve.wait_ge(s_setup_v, 8)
                dve.tensor_copy(bias_parts[64:65, :], bias_rest2[0:1, :]).then_inc(s_setup_v, 1)

            def statistics(w, c, src):
                L, p = ln[w], c.par
                wait_past(dve, ln_shift[w], c.k - 1)
                for t in range(2):
                    last = dve.bn_stats(L["raw"][p][:, t, :], src[p][:, t, :])
                last.then_inc(ln_raw[w], 1)
                dve.wait_ge(ln_raw[w], c.k + 1)
                stand_alone(dve, c)
                for t in range(2):
                    last = dve.bn_aggr(L["stat"][p][:, t, :], L["raw"][p][:, t, :])
                last.then_inc(ln_stat[w], 1)

            def sums(c, t):
                dve.wait_ge(exp_done, 2 * c.k + t + 1)
                wait_past(dve, probs_scaled, 2 * c.k + t - 1)
                dve.tensor_reduce(prob_sum[t][:, :], probs[t][:, :, :], AX.X, ALU.add).then_inc(sum_done, 1)
                dve.wait_ge(sum_done, 2 * c.k + t + 1)
                dve.reciprocal(prob_inv[t][:, :], prob_sum[t][:, :]).then_inc(inv_done, 1)

            def turn_probs(c, t):
                dve.wait_ge(probs_scaled, 2 * c.k + t + 1)
                wait_past(dve, ctx_done, c.k - 1)
                dve.transpose(probs_t[c.par][t][:, :, :], probs_n[t][:, :, :]).then_inc(probs_turned, 1)

            def mask_scores(c, t):
                dve.wait_ge(scores_done, 2 * c.k + t + 1)
                wait_past(dve, scores_shifted, 2 * c.k + t - 1)
                dve.tensor_tensor(scores[t][:, :, :], ps_scores[t],
                                  causal.unsqueeze(1).to_broadcast([128, 16, BLOCK]), ALU.add)\
                   .then_inc(scores_masked, 1)
                dve.wait_ge(scores_masked, 2 * c.k + t + 1)
                dve.tensor_reduce(score_max[t][:, :], scores[t][:, :, :], AX.X, ALU.max).then_inc(max_done, 1)

            def step(chunk_of):
                if (c := chunk_of(CTX)) is not None:
                    sums(c, 0)
                    sums(c, 1)
                if (c := chunk_of(ENTER)) is not None:
                    dve.wait_ge(expert_done, c.k + 1)
                    dve.wait_ge(dom_saved, c.k + 1)
                    wait_past(dve, tok_done, c.k - 1)
                    for a in range(HALVES):
                        last = dve.scalar_tensor_tensor(expert_t[c.par][:, a, :], dom_row[c.par][:, :],
                                                        row_domain[:, a:a + 1], ps_expert[:, a, :],
                                                        ALU.is_equal, ALU.mult)
                    last.then_inc(expert_masked, 1)
                if (c := chunk_of(OUT)) is not None:
                    dve.wait_ge(ffn_done, c.k + 1)
                    wait_past(dve, gate_exp_done, c.k - 1)
                    dve.tensor_reduce(gate_max[c.par][:, :], ps_ffn[:, :, DIM:], AX.X, ALU.max)\
                       .then_inc(gate_max_done, 1)
                    dve.wait_ge(gate_max_done, c.k + 1)
                    dve.tensor_tensor(gate_shift[c.par][:, :, :], ps_ffn[:, :, DIM:],
                                      gate_max[c.par][:, :].unsqueeze(2).to_broadcast([128, 2, N_EXP]),
                                      ALU.subtract).then_inc(gate_shifted, 1)
                if (c := chunk_of(CTX)) is not None:
                    turn_probs(c, 0)
                    turn_probs(c, 1)
                if (c := chunk_of(OUT)) is not None:
                    dve.wait_ge(gate_exp_done, c.k + 1)
                    wait_past(dve, out_saved, 2 * c.k - 2)
                    dve.tensor_reduce(gate_sum[c.par][:, :], gate_exp[c.par][:, :, :], AX.X, ALU.add)\
                       .then_inc(gate_sum_done, 1)
                    dve.wait_ge(gate_sum_done, c.k + 1)
                    dve.reciprocal(gate_best[c.par][:, :], gate_sum[c.par][:, :]).then_inc(gate_ready, 1)
                    dve.wait_ge(gate_ready, c.k + 1)
                    wait_past(dve, out_stored[c.par], 16 * c.pair)
                    for t in range(2):
                        dve.scalar_tensor_tensor(out_sb[c.par][:, t, :], ps_ffn[:, t, 0:DIM],
                                                 gate_best[c.par][:, t:t + 1], h2[c.par][:, t, :],
                                                 ALU.mult, ALU.add).then_inc(out_saved, 1)
                if (c := chunk_of(QKV)) is not None:
                    dve.wait_ge(q_done, c.k + 1)
                    wait_past(dve, scores_done, 2 * c.k - 2)
                    if isinstance(c.k, int) and c.k < 2:
                        dve.wait_ge(s_setup_g, 7)
                    for a in range(HALVES):
                        for s in range(2):
                            rows = slice(64 * s, 64 * s + 64)
                            last = dve.tensor_scalar(q_t[c.par][rows, a, s, :], ps_q[rows, a, :],
                                                     q_scale[rows, a:a + 1], q_bias[rows, a:a + 1],
                                                     ALU.mult, ALU.add)
                    last.then_inc(q_saved, 1)
                    dve.wait_ge(k_saved, c.k + 1)
                    for i in range(4):
                        last = dve.tensor_scalar(k_slots[c.par][:, :, i, :], k_t[c.par][:, :, :],
                                                 slot_mask[:, i:i + 1], None, ALU.mult)
                    last.then_inc(k_spread, 1)
                if (c := chunk_of(CTX)) is not None:
                    dve.wait_ge(attn_done, c.k + 1)
                    wait_past(dve, ln_raw[1], c.k - 1)
                    wait_past(dve, xn2_saved, c.k - 1)
                    wait_past(dve, out_saved, 2 * c.k - 2)
                    dve.tensor_tensor(h2[c.par][:, :, :], ps_attn, h1[c.par][:, :, :], ALU.add)\
                       .then_inc(h2_saved, 1)
                    dve.wait_ge(h2_saved, c.k + 1)
                    statistics(1, c, h2)
                if (c := chunk_of(ENTER)) is not None:
                    dve.wait_ge(tok_done, c.k + 1)
                    dve.wait_ge(base_in[c.par], 32 * c.pair + 32)
                    wait_past(dve, ln_raw[0], c.k - 1)
                    wait_past(dve, xn1_saved, c.k - 1)
                    wait_past(dve, h2_saved, c.k - 1)
                    dve.scalar_tensor_tensor(h1[c.par][:, :, :], ps_tok, 0.1, base[c.par][:, :, :],
                                             ALU.mult, ALU.add).then_inc(h1_saved, 1)
                    dve.wait_ge(h1_saved, c.k + 1)
                    statistics(0, c, h1)
                    if isinstance(c.k, int) and c.k == 0:
                        split_biases()
                if (c := chunk_of(QKV)) is not None:
                    mask_scores(c, 0)
                    mask_scores(c, 1)

            run_steps(dve, step)

        @block.tensor
        def _(pe):
            def turn(src, dst, sem_done):
                for a in range(HALVES):
                    for t in range(2):
                        last = pe.transpose(dst[:, a, t * TILE:(t + 1) * TILE],
                                            src[:, t, a * 128:(a + 1) * 128], ident)
                last.then_inc(sem_done, 1)

            def features_out(dst, weight, src_t, sem_done):
                for m in range(HALVES):
                    for a in range(HALVES):
                        last = pe.matmul(dst[:, m, :], weight[:, a, m * 128:(m + 1) * 128], src_t[:, a, :],
                                         start=(a == 0), stop=(a == HALVES - 1))
                last.then_inc(sem_done, 1)

            def tokens_out(dst, src_t, weight, sem_done, bias=None):
                for t in range(2):
                    for a in range(HALVES):
                        last = pe.matmul(dst[:, t, :], src_t[:, a, t * TILE:(t + 1) * TILE], weight[:, a, :],
                                         start=(a == 0), stop=(a == HALVES - 1 and bias is None))
                    if bias is not None:
                        last = pe.matmul(dst[:, t, :], ones_bf[:, :], bias, start=False, stop=True)
                last.then_inc(sem_done, 1)

            def bring_in(c):
                if isinstance(c.k, int) and c.k == 0:
                    pe.wait_ge(s_consts, 16)
                    pe.wait_ge(s_setup_v, 1)
                pe.wait_ge(base_in[c.par], 32 * c.pair + 32)
                wait_past(pe, ctx_saved, c.k - 2)
                wait_past(pe, base_t_saved, c.k)
                turn(base[c.par], ps_base_t, base_turned)
                pe.wait_ge(dom_cast, c.k + 1)
                wait_past(pe, v_saved, c.k - 1)
                wait_past(pe, dom_saved, c.k)
                for t in range(2):
                    last = pe.matmul(ps_dom[:, t * TILE:(t + 1) * TILE],
                                     dom_bf[c.par][:, t:t + 1].to_broadcast([128, 128]), ident_bf[:, :],
                                     start=True, stop=True)
                last.then_inc(dom_spread, 1)

            def step(chunk_of):
                if (c := chunk_of(QKV)) is not None:
                    pe.wait_ge(xn1_saved, c.k + 1)
                    wait_past(pe, h2_saved, c.k - 1)
                    turn(xn1[c.par], ps_xn1_t, xn1_turned)
                if (c := chunk_of(ENTER)) is not None:
                    if isinstance(c.k, int) and c.k == 0:
                        pe.wait_ge(s_wexp, 16)
                    pe.wait_ge(base_t_saved, c.k + 1)
                    wait_past(pe, expert_masked, c.k)
                    wait_past(pe, xn2_t_saved, c.k - 3)
                    features_out(ps_expert, w_exp_sb, base_t[c.par], expert_done)
                if (c := chunk_of(QKV)) is not None:
                    if isinstance(c.k, int) and c.k == 0:
                        pe.wait_ge(s_qkvw, 16 * 3)
                    pe.wait_ge(xn1_t_saved, c.k + 1)
                    wait_past(pe, scores_masked, 2 * c.k)
                    features_out(ps_q, wq_sb, xn1_t[c.par], q_done)
                    features_out(ps_k, wk_sb, xn1_t[c.par], k_done)
                if (c := chunk_of(CTX)) is not None:
                    pe.wait_ge(v_moved[c.par], 256 * c.pair + 256)
                    pe.wait_ge(probs_turned, 2 * c.k + 2)
                    pe.wait_ge(base_t_saved, at_most_all(c.k + 3))
                    for t in range(2):
                        for b in range(BLOCKS):
                            for i in range(4):
                                last = pe.matmul(
                                    ps_ctx[64 * (i % 2):64 * (i % 2) + 64, i // 2,
                                           t * TILE + b * BLOCK:t * TILE + (b + 1) * BLOCK],
                                    v_diag[c.par][:, t, b, i::4],
                                    probs_t[c.par][t][:, 4 * b + i, :], start=True, stop=True)
                    last.then_inc(ctx_done, 1)
                if (c := chunk_of(QKV)) is not None:
                    pe.wait_ge(dom_saved, at_most_all(c.k + 2))
                    tokens_out(ps_v, xn1_t[c.par], wv_sb, v_done)
                if (c := chunk_of(CTX)) is not None:
                    pe.wait_ge(ctx_saved, c.k + 1)
                    if isinstance(c.k, int) and c.k == 0:
                        pe.wait_ge(s_setup_v, 9)
                    pe.wait_ge(xn1_t_saved, at_most_all(c.k + 2))
                    tokens_out(ps_attn, ctx_t[c.par], wo_sb, attn_done, bias_parts[:, 0:DIM])
                if (c := chunk_of(ENTER)) is not None:
                    if isinstance(c.k, int) and c.k == 0:
                        pe.wait_ge(s_wproj, 16)
                    pe.wait_ge(expert_masked, c.k + 1)
                    wait_past(pe, h1_saved, c.k)
                    wait_past(pe, out_saved, 2 * (c.k - 3))
                    tokens_out(ps_tok, expert_t[c.par], w_proj_sb, tok_done)
                if (c := chunk_of(FFN)) is not None:
                    pe.wait_ge(xn2_saved, c.k + 1)
                    pe.wait_ge(expert_masked, at_most_all(c.k + 4))
                    turn(xn2[c.par], ps_xn2_t, xn2_turned)
                if (c := chunk_of(QKV)) is not None:
                    pe.wait_ge(q_saved, c.k + 1)
                    pe.wait_ge(k_spread, c.k + 1)
                    for t in range(2):
                        for b in range(BLOCKS):
                            cols = slice(t * TILE + b * BLOCK, t * TILE + (b + 1) * BLOCK)
                            for u in range(4):
                                last = pe.matmul(ps_scores[t][32 * u:32 * u + 32, 4 * b:4 * b + 4, :],
                                                 q_t[c.par][:, u // 2, u % 2, cols],
                                                 k_slots[c.par][:, u // 2, :, cols], start=True, stop=True)
                        last.then_inc(scores_done, 1)
                if (c := chunk_of(LEAD_IN)) is not None:
                    bring_in(c)
                    if isinstance(c.k, int) and c.k == 0:
                        pe.wait_ge(s_wof, 16 * 3)
                        for a in range(HALVES):
                            last = pe.matmul(ps[0:1, 5, 0:DIM], bv_sb[:, a:a + 1], wo_sb[:, a, :],
                                             start=(a == 0), stop=(a == HALVES - 1))
                        last.then_inc(s_setup_p, 1)
                if (c := chunk_of(FFN)) is not None:
                    pe.wait_ge(xn2_t_saved, c.k + 1)
                    wait_past(pe, out_saved, 2 * c.k)
                    pe.wait_ge(h1_saved, at_most_all(c.k + 4))
                    tokens_out(ps_ffn, xn2_t[c.par], wf_sb, ffn_done, bias_parts[:, DIM:])

            run_steps(pe, step)


def lay_out_constants():
    import numpy as np
    c = np.zeros((128, C_END), np.float32)
    p = np.arange(128)
    c[:, C_IDENT:C_IDENT + 128] = np.eye(128)
    query, key = (p % BLOCK)[:, None], np.arange(BLOCK)[None, :]
    seen = (query // 16 == key // 16) & (key <= query)
    c[:, C_MASK:C_MASK + BLOCK] = np.where(seen, 0.0, -1e30)
    c[:, C_SLOT:C_SLOT + 4] = (p // D_HEAD % 4)[:, None] == np.arange(4)[None, :]
    c[:, C_DOMAIN:C_DOMAIN + 2] = (p[:, None] + 128 * np.arange(2)[None, :]) // EXPAND
    return c


def kernel(**inputs):
    import numpy as np
    import concourse.bacc as bacc
    from concourse.bass_utils import run_bass_kernel_spmd

    a = {k: np.asarray(v) for k, v in inputs.items()}
    order = a["x"].reshape(SEQ // DILATION, DILATION, BATCH).transpose(2, 1, 0).reshape(N_CHUNK, 2, 128)
    in_ctx_order = a["L0_attn_Wo"].T.reshape(4, 4, D_HEAD, DIM).transpose(1, 0, 2, 3).reshape(DIM, DIM)
    bv_in_ctx_order = a["L0_attn_bv"].reshape(4, 4, D_HEAD).transpose(1, 0, 2).reshape(DIM)
    wv_in_quad_order = a["L0_attn_Wv"].T.reshape(DIM, 4, 4, D_HEAD).transpose(0, 1, 3, 2).reshape(DIM, DIM)
    per_feature = [a["L0_attn_bq"], a["L0_attn_bk"], bv_in_ctx_order, np.repeat(a["L0_attn_beta"], D_HEAD)]
    arrays = {
        "ids": order.transpose(0, 2, 1).reshape(N_CHUNK * 128, 2),
        "domain_map": a["L0_tok_domain_map"].reshape(VOCAB, 1),
        "emb_table": a["L0_tok_emb_table"],
        "w_exp": a["L0_tok_W_exp"].reshape(DIM, DIM).T,
        "w_proj": a["L0_tok_W_proj"].transpose(0, 2, 1).reshape(DIM, DIM),
        "wq": a["L0_attn_Wq"].T, "wk": a["L0_attn_Wk"].T, "wv": wv_in_quad_order, "wo": in_ctx_order,
        "columns": np.stack([x.reshape(HALVES, 128).T for x in per_feature], 1),
        "bo": a["L0_attn_bo"],
        "wg": a["L0_ffn_Wg"], "bg": a["L0_ffn_bg"], "we": a["L0_ffn_We"], "be": a["L0_ffn_be"],
        "consts": lay_out_constants(),
    }
    arrays = {k: np.ascontiguousarray(v) for k, v in arrays.items()}
    nc = bacc.Bacc("TRN2", target_bir_lowering=False, num_devices=1)
    args = {k: nc.dram_tensor(k, v.shape, mybir.dt.from_np(v.dtype), kind="ExternalInput").ap()
            for k, v in arrays.items()}
    out = nc.dram_tensor("out", (TOKENS, DIM), FP32, kind="ExternalOutput").ap()
    build_lm_tower(nc, out=out, **args)
    r = run_bass_kernel_spmd(nc, [arrays], core_ids=[0])
    got = np.asarray(r.results[0]["out"])
    return got.reshape(BATCH, DILATION, SEQ // DILATION, DIM).transpose(2, 1, 0, 3).reshape(SEQ, BATCH, DIM)
```

```python
import concourse.bass as bass
from concourse import mybir
from contextlib import ExitStack

FP32 = mybir.dt.float32
BF16 = mybir.dt.bfloat16
FP32R = mybir.dt.float32r
INT32 = mybir.dt.int32
ALU = mybir.AluOpType
ACT = mybir.ActivationFunctionType
AX = mybir.AxisListType

SEQ, BATCH = 64, 128
DIM = 256
VOCAB = 50257
N_DOM, EXPAND = 8, 32
HEADS, D_HEAD = 16, 16
DILATION = 4
N_EXP = 8
LN_EPS = 1e-5

TOKENS = SEQ * BATCH
TILE = 128
CHUNK = 2 * TILE
N_CHUNK = TOKENS // CHUNK
BLOCK = 32
BLOCKS = TILE // BLOCK
HALVES = DIM // 128
QUAD_HEADS = HEADS // 4

C_IDENT, C_MASK, C_SLOT, C_DOMAIN, C_END = 0, 128, 160, 164, 166


class Chunk:

    def __init__(self, offset, j=None):
        self.par = offset % 2
        self.quad = offset % 4
        self.k = offset if j is None else 4 * j + offset
        self.pair = offset // 2 if j is None else 2 * j + offset // 2


IDS_LAG, LAST_LAG = -2, 5
LOOP_FROM, LOOP_TO = 8, 28


def run_steps(engine, step):

    def peeled(n):
        step(lambda lag: Chunk(n - lag) if 0 <= n - lag < N_CHUNK else None)

    for n in range(LOOP_FROM):
        peeled(n)
    with engine.Fori(0, (LOOP_TO - LOOP_FROM) // 4) as j:
        for s in range(4):
            step(lambda lag: Chunk(LOOP_FROM + s - lag, j))
    for n in range(LOOP_TO, N_CHUNK + LAST_LAG):
        peeled(n)


def is_first(c):
    return isinstance(c.k, int) and c.k == 0


def wait_past(engine, sem, count):
    if not isinstance(count, int) or count > 0:
        engine.wait_ge(sem, count)


def at_most_all(count, per_chunk=1):
    return min(count, per_chunk * N_CHUNK) if isinstance(count, int) else count


def build_lm_tower(nc, ids, domain_map, emb_table, w_exp, w_proj, wq, wk, wv, wo, bo, wg, bg, we, be,
                   columns, consts, out):
    ctx = ExitStack()
    with ctx:
        def sb(name, shape, dt=FP32):
            return ctx.enter_context(nc.sbuf_tensor(name, shape, dt))

        def sem(name):
            return ctx.enter_context(nc.semaphore(name))

        const_sb = sb("const_sb", [128, C_END])
        ident = const_sb[:, C_IDENT:C_IDENT + 128]
        causal = const_sb[:, C_MASK:C_MASK + BLOCK]
        slot_mask = const_sb[:, C_SLOT:C_SLOT + 4]
        row_domain = const_sb[:, C_DOMAIN:C_DOMAIN + 2]
        ident_bf = sb("ident_bf", [128, 128], BF16)
        mask_bf = sb("mask_bf", [128, 16, BLOCK], BF16)
        ones_bf = sb("ones_bf", [128, 128], BF16)
        w_exp_sb = sb("w_exp_sb", [128, HALVES, DIM])
        w_proj_sb = sb("w_proj_sb", [128, HALVES, DIM])
        wq_sb = sb("wq_sb", [128, HALVES, DIM])
        wk_sb = sb("wk_sb", [128, HALVES, DIM])
        wv_sb = sb("wv_sb", [128, HALVES, DIM])
        wo_sb = sb("wo_sb", [128, HALVES, DIM])
        wf_sb = sb("wf_sb", [128, HALVES, DIM + N_EXP])
        columns_sb = sb("columns_sb", [128, 4, HALVES])
        bq_sb, bk_sb, bv_sb, beta_sb = (columns_sb[:, n, :] for n in range(4))
        q_scale = sb("q_scale", [128, HALVES])
        q_bias = sb("q_bias", [128, HALVES])
        N_BIAS = 2 * DIM + N_EXP
        parts_of = {name: [sb(f"{name}_{part}", [128, HALVES, width], FP32R) for part in ("hi", "lo")]
                    for name, width in (("wq", DIM), ("wk", DIM), ("wv", DIM), ("wo", DIM), ("wf", DIM + N_EXP))}
        bias_row = sb("bias_row", [1, N_BIAS])
        bias_rest = sb("bias_rest", [1, N_BIAS])
        bias_rest2 = sb("bias_rest2", [1, N_BIAS])
        bias_parts = sb("bias_parts", [128, N_BIAS], BF16)
        minus_half = sb("minus_half", [128, 2])
        minus_one = sb("minus_one", [128, 2])
        eps = sb("eps", [128, 2])

        def pair(name, shape, dt=FP32):
            return [sb(f"{name}{p}", shape, dt) for p in range(2)]

        id_sb = pair("id_sb", [128, 2], INT32)
        dom_int = pair("dom_int", [128, 2], INT32)
        dom_bf = pair("dom_bf", [128, 2], BF16)
        def four(name, shape, dt=FP32):
            return [sb(f"{name}{p}", shape, dt) for p in range(4)]

        base = pair("base", [128, 2, DIM])
        base_t = pair("base_t", [128, HALVES, CHUNK])
        dom_row = pair("dom_row", [128, CHUNK])
        expert_t = pair("expert_t", [128, HALVES, CHUNK])
        h1 = four("h1", [128, 2, DIM])
        xn1 = pair("xn1", [128, 2, DIM])
        xn1_hi = pair("xn1_hi", [128, HALVES, CHUNK], FP32R)
        xn1_lo = pair("xn1_lo", [128, HALVES, CHUNK], FP32R)
        q_t = pair("q_t", [128, HALVES, CHUNK])
        k_t = pair("k_t", [128, HALVES, CHUNK])
        k_slots = pair("k_slots", [128, HALVES, 4, CHUNK])
        v_diag = pair("v_diag", [128, 2, BLOCKS, DIM])
        scores = pair("scores", [128, 16, BLOCK])
        shifted = pair("shifted", [128, 16, BLOCK])
        probs = pair("probs", [128, 16, BLOCK])
        probs_n = pair("probs_n", [128, 16, BLOCK])
        probs_t = [[sb(f"probs_t{p}{t}", [128, 16, BLOCK]) for t in range(2)] for p in range(2)]
        score_max = pair("score_max", [128, 16])
        prob_sum = pair("prob_sum", [128, 16])
        prob_inv = pair("prob_inv", [128, 16])
        ctx_hi = pair("ctx_hi", [128, HALVES, CHUNK], FP32R)
        ctx_lo = pair("ctx_lo", [128, HALVES, CHUNK], FP32R)
        h2 = four("h2", [128, 2, DIM])
        xn2 = pair("xn2", [128, 2, DIM])
        xn2_hi = pair("xn2_hi", [128, HALVES, CHUNK], FP32R)
        xn2_lo = pair("xn2_lo", [128, HALVES, CHUNK], FP32R)
        out_sb = pair("out_sb", [128, 2, DIM])
        gate_max = pair("gate_max", [128, 2])
        gate_shift = pair("gate_shift", [128, 2, N_EXP])
        gate_exp = pair("gate_exp", [128, 2, N_EXP])
        gate_sum = pair("gate_sum", [128, 2])
        gate_best = pair("gate_best", [128, 2])
        ln = []
        for w in (1, 2):
            ln.append(dict(
                raw=pair(f"ln{w}_raw", [128, 2, 6]), stat=pair(f"ln{w}_stat", [128, 2, 2]),
                var=pair(f"ln{w}_var", [128, 2]), rstd=pair(f"ln{w}_rstd", [128, 2]),
                mr=pair(f"ln{w}_mr", [128, 2]), shift=pair(f"ln{w}_shift", [128, 2])))

        ps = ctx.enter_context(nc.psum_tensor("ps", [128, 8, 512], FP32))

        def halves(bank):
            return ps[:, bank, :].rearrange("p (a n) -> p a n", a=2)

        ps_scores = [ps[:, t, :].rearrange("p (m t) -> p m t", t=BLOCK) for t in range(2)]
        ps_q = halves(0)
        ps_xn1_t, ps_v = halves(1), halves(1)
        ps_k, ps_xn2_t = halves(2), halves(2)
        ps_dom, ps_ctx = ps[:, 3, 0:CHUNK], halves(3)
        ps_ffn = ps[:, 4:6, 0:DIM + N_EXP]
        ps_attn = halves(4)
        ps_wo_bv = ps[0:1, 5, 0:DIM]
        ps_base_t, ps_tok = halves(6), halves(6)
        ps_expert = halves(7)

        s_consts, s_wexp, s_wproj, s_qkvw, s_wof, s_rows, s_columns = (
            sem(n) for n in ("consts_in", "wexp_in", "wproj_in", "qkv_weights_in", "wo_wffn_in", "bias_rows_in",
                             "columns_in"))
        s_passed = sem("passed")
        s_setup_v, s_setup_g, s_setup_a, s_setup_p = (sem(n) for n in ("setup_vector", "setup_pool", "setup_act",
                                                                       "setup_pe"))
        v_diag_cleared, weights_hi, weights_lo = (sem(n) for n in ("v_diag_cleared", "weights_hi", "weights_lo"))
        ids_in, base_in, dom_in, out_stored = ([sem(f"{n}{p}") for p in range(2)]
                                               for n in ("ids_in", "base_in", "dom_in", "out_stored"))
        dom_cast = sem("dom_cast")
        base_turned, dom_spread, expert_done, tok_done, xn1_turned = (
            sem(n) for n in ("base_turned", "dom_spread", "expert_done", "tok_done", "xn1_turned"))
        q_done, k_done, v_done, attn_done, xn2_turned, ffn_done = (
            sem(n) for n in ("q_done", "k_done", "v_done", "attn_done", "xn2_turned", "ffn_done"))
        scores_done, scores_saved, max_done, scores_shifted, exp_done, sum_done, inv_done, probs_scaled, \
            probs_turned, ctx_done = (
                [sem(f"{n}{t}") for t in range(2)]
                for n in ("scores_done", "scores_saved", "max_done", "scores_shifted", "exp_done", "sum_done",
                          "inv_done", "probs_scaled", "probs_turned", "ctx_done"))
        base_t_saved, dom_saved, xn1_saved, xn1_hi_saved, k_saved, q_saved, v_saved, ctx_hi_saved, xn2_saved, \
            xn2_hi_saved, gate_exp_done = (
                sem(n) for n in ("base_t_saved", "dom_saved", "xn1_saved", "xn1_hi_saved", "k_saved", "q_saved",
                                 "v_saved", "ctx_hi_saved", "xn2_saved", "xn2_hi_saved", "gate_exp_done"))
        expert_masked, h1_saved, xn1_lo_saved, k_spread, ctx_lo_saved, h2_saved, xn2_lo_saved, gate_max_done, \
            gate_shifted, gate_sum_done, gate_ready, out_saved = (
                sem(n) for n in ("expert_masked", "h1_saved", "xn1_lo_saved", "k_spread", "ctx_lo_saved",
                                 "h2_saved", "xn2_lo_saved", "gate_max_done", "gate_shifted", "gate_sum_done",
                                 "gate_ready", "out_saved"))
        ln_raw = [sem(f"ln{w}_raw_done") for w in (1, 2)]
        ln_stat = [sem(f"ln{w}_stat_done") for w in (1, 2)]
        ln_var = [sem(f"ln{w}_var_done") for w in (1, 2)]
        ln_rstd = [sem(f"ln{w}_rstd_done") for w in (1, 2)]
        ln_mr = [sem(f"ln{w}_mr_done") for w in (1, 2)]
        ln_shift = [sem(f"ln{w}_shift_done") for w in (1, 2)]

        def stand_alone(engine, c):
            if not isinstance(c.k, int):
                engine.sem_inc(s_passed, 1)

        ids_by_chunk = ids.rearrange("(c p) t -> c p t", p=128)
        out_by_chunk = out.rearrange("(c t p) f -> c p t f", t=2, p=128)
        block = ctx.enter_context(nc.Block())

        @block.sync
        def _(sp):
            def load_ids(c):
                wait_past(sp, base_in[c.par], 32 * c.pair)
                wait_past(sp, dom_in[c.par], 32 * c.pair)
                stand_alone(sp, c)
                sp.dma_start(id_sb[c.par][:, :], ids_by_chunk[c.k]).then_inc(ids_in[c.par], 16)

            load_ids(Chunk(0))
            load_ids(Chunk(1))
            sp.dma_start(const_sb[:, :], consts).then_inc(s_consts, 16)
            sp.dma_start(columns_sb[:, :, :], columns).then_inc(s_columns, 16)
            sp.dma_start(w_exp_sb[:, :, :], w_exp.rearrange("(a p) m -> p a m", p=128)).then_inc(s_wexp, 16)
            sp.dma_start(w_proj_sb[:, :, :], w_proj.rearrange("(a p) m -> p a m", p=128)).then_inc(s_wproj, 16)
            for w, dst in ((wq, wq_sb), (wk, wk_sb), (wv, wv_sb)):
                sp.dma_start(dst[:, :, :], w.rearrange("(a p) m -> p a m", p=128)).then_inc(s_qkvw, 16)
            sp.dma_start(wo_sb[:, :, :], wo.rearrange("(a p) m -> p a m", p=128)).then_inc(s_wof, 16)
            sp.dma_start(wf_sb[:, :, 0:DIM], we.rearrange("(a p) m -> p a m", p=128)).then_inc(s_wof, 16)
            sp.dma_start(wf_sb[:, :, DIM:], wg.rearrange("(a p) m -> p a m", p=128)).then_inc(s_wof, 16)
            for b, at, n in ((bo, 0, DIM), (be, DIM, DIM), (bg, 2 * DIM, N_EXP)):
                sp.dma_start(bias_row[0:1, at:at + n], b.rearrange("(a n) -> a n", a=1)).then_inc(s_rows, 16)

            def step(chunk_of):
                if (c := chunk_of(LAST_LAG)) is not None:
                    sp.wait_ge(out_saved, 2 * c.k + 2)
                    stand_alone(sp, c)
                    sp.dma_start(out_by_chunk[c.k], out_sb[c.par][:, :, :]).then_inc(out_stored[c.par], 16)
                if (c := chunk_of(IDS_LAG)) is not None:
                    load_ids(c)

            run_steps(sp, step)
            for p in range(2):
                sp.wait_ge(out_stored[p], 16 * (N_CHUNK // 2))

        @block.gpsimd
        def _(pool):
            def gather(c):
                pool.wait_ge(ids_in[c.par], 16 * c.pair + 16)
                wait_past(pool, h1_saved, c.k - 1)
                wait_past(pool, dom_cast, c.k - 1)
                stand_alone(pool, c)
                for t in range(2):
                    pool.indirect_dma_start(base[c.par][:, t, :], None, emb_table,
                                            bass.IndirectOffsetOnAxis(id_sb[c.par][:, t:t + 1], 0))\
                        .then_inc(base_in[c.par], 16)
                    pool.indirect_dma_start(dom_int[c.par][:, t:t + 1], None, domain_map,
                                            bass.IndirectOffsetOnAxis(id_sb[c.par][:, t:t + 1], 0))\
                        .then_inc(dom_in[c.par], 16)

            def cast_domains(c):
                pool.wait_ge(dom_in[c.par], 32 * c.pair + 32)
                wait_past(pool, dom_spread, c.k - 1)
                stand_alone(pool, c)
                pool.tensor_copy(dom_bf[c.par][:, :], dom_int[c.par][:, :]).then_inc(dom_cast, 1)

            def layernorm_scalars(w, c):
                L, p = ln[w], c.par
                pool.wait_ge(ln_stat[w], c.k + 1)
                wait_past(pool, xn1_saved if w == 0 else xn2_saved, c.k - 1)
                pool.tensor_tensor(L["var"][p][:, :], L["stat"][p][:, :, 1], eps[:, :], ALU.add)\
                    .then_inc(ln_var[w], 1)
                pool.wait_ge(ln_var[w], c.k + 1)
                pool.tensor_tensor(L["rstd"][p][:, :], L["var"][p][:, :], minus_half[:, :], ALU.pow)\
                    .then_inc(ln_rstd[w], 1)
                pool.wait_ge(ln_rstd[w], c.k + 1)
                pool.tensor_tensor(L["mr"][p][:, :], L["stat"][p][:, :, 0], L["rstd"][p][:, :], ALU.mult)\
                    .then_inc(ln_mr[w], 1)
                pool.wait_ge(ln_mr[w], c.k + 1)
                pool.tensor_tensor(L["shift"][p][:, :], L["mr"][p][:, :], minus_one[:, :], ALU.mult)\
                    .then_inc(ln_shift[w], 1)

            def shift_scores(c, t):
                pool.wait_ge(max_done[t], c.k + 1)
                wait_past(pool, exp_done[t], c.k)
                pool.tensor_tensor(shifted[t][:, :, :], scores[t][:, :, :],
                                   score_max[t][:, :].unsqueeze(2).to_broadcast([128, 16, BLOCK]),
                                   ALU.subtract).then_inc(scores_shifted[t], 1)

            def scale_probs(c, t):
                pool.wait_ge(inv_done[t], c.k + 1)
                wait_past(pool, probs_turned[t], c.k)
                pool.tensor_tensor(probs_n[t][:, :, :], probs[t][:, :, :],
                                   prob_inv[t][:, :].unsqueeze(2).to_broadcast([128, 16, BLOCK]),
                                   ALU.mult).then_inc(probs_scaled[t], 1)

            for tile, value in ((minus_half, -0.5), (minus_one, -1.0), (eps, LN_EPS)):
                pool.memset(tile[:, :], value).then_inc(s_setup_g, 1)
            pool.wait_ge(s_setup_g, 3)

            def step(chunk_of):
                if (c := chunk_of(0)) is not None:
                    gather(c)
                    cast_domains(c)
                if (c := chunk_of(1)) is not None:
                    layernorm_scalars(0, c)
                if (c := chunk_of(2)) is not None:
                    shift_scores(c, 1)
                    shift_scores(c, 0)
                if (c := chunk_of(3)) is not None:
                    layernorm_scalars(1, c)
                if (c := chunk_of(2)) is not None:
                    scale_probs(c, 1)
                    scale_probs(c, 0)

            run_steps(pool, step)

        @block.scalar
        def _(act):
            act.wait_ge(s_columns, 16)
            act.activation(q_scale[:, :], beta_sb[:, :], ACT.Exp, scale=-1.0).then_inc(s_setup_a, 1)

            def round_weights(names, sbs, arrived, count):
                act.wait_ge(arrived, count)
                for name, w_sb in zip(names, sbs):
                    act.activation(parts_of[name][0][:, :, :], w_sb[:, :, :], ACT.Copy).then_inc(weights_hi, 1)

            def save_base_t(c):
                act.wait_ge(base_turned, c.k + 1)
                wait_past(act, expert_done, c.k - 1)
                act.activation(base_t[c.par][:, :, :], ps_base_t, ACT.Copy).then_inc(base_t_saved, 1)

            def save_domains(c):
                act.wait_ge(dom_spread, c.k + 1)
                wait_past(act, expert_masked, c.k - 1)
                act.activation(dom_row[c.par][:, :], ps_dom, ACT.Copy).then_inc(dom_saved, 1)

            def normalise(w, c, src, dst, saved, turned):
                L, p = ln[w], c.par
                act.wait_ge(ln_shift[w], c.k + 1)
                wait_past(act, turned, c.k - 1)
                for t in range(2):
                    last = act.activation(dst[p][:, t, :], src[:, t, :], ACT.Identity,
                                          scale=L["rstd"][p][:, t:t + 1], bias=L["shift"][p][:, t:t + 1])
                last.then_inc(saved, 1)

            def save_hi(c, psum, hi, produced, saved, used):
                act.wait_ge(produced, c.k + 1)
                wait_past(act, used, c.k - 1)
                act.activation(hi[c.par][:, :, :], psum, ACT.Copy).then_inc(saved, 1)

            def save_k(c):
                act.wait_ge(k_done, c.k + 1)
                wait_past(act, k_spread, c.k - 1)
                for a in range(HALVES):
                    last = act.activation(k_t[c.par][:, a, :], ps_k[:, a, :], ACT.Identity,
                                          bias=bk_sb[:, a:a + 1])
                last.then_inc(k_saved, 1)

            def save_q(c):
                act.wait_ge(q_done, c.k + 1)
                if is_first(c):
                    act.wait_ge(s_setup_v, 3)
                for t in range(2):
                    wait_past(act, scores_done[t], c.k - 1)
                for a in range(HALVES):
                    last = act.activation(q_t[c.par][:, a, :], ps_q[:, a, :], ACT.Identity,
                                          scale=q_scale[:, a:a + 1], bias=q_bias[:, a:a + 1])
                last.then_inc(q_saved, 1)

            def save_v_diagonal(c):
                act.wait_ge(v_done, c.k + 1)
                for t in range(2):
                    wait_past(act, ctx_done[t], c.k - 1)
                if is_first(c):
                    act.wait_ge(v_diag_cleared, 2)
                for b in range(BLOCKS):
                    for u in range(4):
                        last = act.activation(v_diag[c.par][32 * u:32 * u + 32, :, b, 64 * u:64 * u + 64],
                                              ps_v[32 * b:32 * b + 32, :, 64 * u:64 * u + 64], ACT.Copy)
                last.then_inc(v_saved, 1)

            def save_scores(c, t):
                act.wait_ge(scores_done[t], c.k + 1)
                wait_past(act, scores_shifted[t], c.k)
                act.activation(scores[t][:, :, :], ps_scores[t], ACT.Copy).then_inc(scores_saved[t], 1)

            def exponentials(c, t):
                act.wait_ge(scores_shifted[t], c.k + 1)
                wait_past(act, probs_scaled[t], c.k)
                act.activation(probs[t][:, :, :], shifted[t][:, :, :], ACT.Exp).then_inc(exp_done[t], 1)

            def step(chunk_of):
                if (c := chunk_of(2)) is not None:
                    save_q(c)
                if (c := chunk_of(3)) is not None:
                    act.wait_ge(ctx_done[1], c.k + 1)
                    save_hi(c, ps_ctx, ctx_hi, ctx_done[0], ctx_hi_saved, attn_done)
                if (c := chunk_of(4)) is not None:
                    save_hi(c, ps_xn2_t, xn2_hi, xn2_turned, xn2_hi_saved, ffn_done)
                if (c := chunk_of(2)) is not None:
                    save_scores(c, 1)
                    save_scores(c, 0)
                if (c := chunk_of(0)) is not None:
                    save_base_t(c)
                    save_domains(c)
                    if is_first(c):
                        round_weights(("wq", "wk", "wv"), (wq_sb, wk_sb, wv_sb), s_qkvw, 16 * 3)
                if (c := chunk_of(1)) is not None:
                    normalise(0, c, h1[c.quad], xn1, xn1_saved, xn1_turned)
                if (c := chunk_of(2)) is not None:
                    exponentials(c, 1)
                if (c := chunk_of(1)) is not None:
                    save_hi(c, ps_xn1_t, xn1_hi, xn1_turned, xn1_hi_saved, v_done)
                if (c := chunk_of(2)) is not None:
                    exponentials(c, 0)
                if (c := chunk_of(3)) is not None:
                    normalise(1, c, h2[c.quad], xn2, xn2_saved, xn2_turned)
                if (c := chunk_of(1)) is not None:
                    save_k(c)
                if (c := chunk_of(4)) is not None:
                    act.wait_ge(gate_shifted, c.k + 1)
                    wait_past(act, gate_sum_done, c.k - 1)
                    act.activation(gate_exp[c.par][:, :, :], gate_shift[c.par][:, :, :], ACT.Exp)\
                       .then_inc(gate_exp_done, 1)
                if (c := chunk_of(1)) is not None:
                    save_v_diagonal(c)
                    if is_first(c):
                        round_weights(("wo", "wf"), (wo_sb, wf_sb), s_wof, 16 * 3)

            run_steps(act, step)

        @block.vector
        def _(dve):
            dve.wait_ge(s_consts, 16)
            dve.tensor_copy(ident_bf[:, :], ident)
            dve.memset(ones_bf[:, :], 1.0)
            dve.tensor_copy(mask_bf[:, :, :], causal.unsqueeze(1).to_broadcast([128, 16, BLOCK]))
            dve.memset(bias_parts[:, :], 0.0).then_inc(s_setup_v, 1)
            dve.wait_ge(s_setup_a, 1)
            dve.tensor_scalar(q_scale[:, :], q_scale[:, :], float(D_HEAD) ** -0.5, None, ALU.mult)\
               .then_inc(s_setup_v, 1)
            dve.wait_ge(s_setup_v, 2)
            dve.tensor_tensor(q_bias[:, :], bq_sb[:, :], q_scale[:, :], ALU.mult).then_inc(s_setup_v, 1)
            for p in range(2):
                dve.memset(v_diag[p][:, :, :, :], 0.0).then_inc(v_diag_cleared, 1)

            def split_biases():
                dve.wait_ge(s_setup_p, 1)
                dve.wait_ge(s_rows, 16 * 3)
                dve.tensor_tensor(bias_row[0:1, 0:DIM], ps_wo_bv, bias_row[0:1, 0:DIM], ALU.add)\
                   .then_inc(s_setup_v, 1)
                dve.wait_ge(s_setup_v, 4)
                dve.tensor_copy(bias_parts[0:1, :], bias_row[0:1, :]).then_inc(s_setup_v, 1)
                dve.wait_ge(s_setup_v, 5)
                dve.tensor_tensor(bias_rest[0:1, :], bias_row[0:1, :], bias_parts[0:1, :], ALU.subtract)\
                   .then_inc(s_setup_v, 1)
                dve.wait_ge(s_setup_v, 6)
                dve.tensor_copy(bias_parts[32:33, :], bias_rest[0:1, :])
                dve.tensor_copy(bias_row[0:1, :].bitcast(BF16)[:, 0:N_BIAS], bias_rest[0:1, :])\
                   .then_inc(s_setup_v, 1)
                dve.wait_ge(s_setup_v, 7)
                dve.tensor_tensor(bias_rest2[0:1, :], bias_rest[0:1, :],
                                  bias_row[0:1, :].bitcast(BF16)[:, 0:N_BIAS], ALU.subtract)\
                   .then_inc(s_setup_v, 1)
                dve.wait_ge(s_setup_v, 8)
                dve.tensor_copy(bias_parts[64:65, :], bias_rest2[0:1, :]).then_inc(s_setup_v, 1)

            def split_weights(names, sbs, done_before):
                for n, (name, w_sb) in enumerate(zip(names, sbs)):
                    hi, lo = parts_of[name]
                    dve.wait_ge(weights_hi, done_before + n + 1)
                    dve.tensor_tensor(lo[:, :, :], w_sb[:, :, :], hi[:, :, :].bitcast(FP32), ALU.subtract)\
                       .then_inc(weights_lo, 1)

            def save_lo(c, psum, hi, lo, hi_saved, saved, used):
                dve.wait_ge(hi_saved, c.k + 1)
                wait_past(dve, used, c.k - 1)
                dve.tensor_tensor(lo[c.par][:, :, :], psum, hi[c.par][:, :, :].bitcast(FP32), ALU.subtract)\
                   .then_inc(saved, 1)

            def statistics(w, c, src):
                L, p = ln[w], c.par
                dve.wait_ge(h1_saved if w == 0 else h2_saved, c.k + 1)
                wait_past(dve, ln_shift[w], c.k - 1)
                for t in range(2):
                    last = dve.bn_stats(L["raw"][p][:, t, :], src[:, t, :])
                last.then_inc(ln_raw[w], 1)
                dve.wait_ge(ln_raw[w], c.k + 1)
                stand_alone(dve, c)
                for t in range(2):
                    last = dve.bn_aggr(L["stat"][p][:, t, :], L["raw"][p][:, t, :])
                last.then_inc(ln_stat[w], 1)

            def mask_experts(c):
                dve.wait_ge(expert_done, c.k + 1)
                dve.wait_ge(dom_saved, c.k + 1)
                wait_past(dve, tok_done, c.k - 1)
                for a in range(HALVES):
                    last = dve.scalar_tensor_tensor(expert_t[c.par][:, a, :], dom_row[c.par][:, :],
                                                    row_domain[:, a:a + 1], ps_expert[:, a, :],
                                                    ALU.is_equal, ALU.mult)
                last.then_inc(expert_masked, 1)

            def first_residual(c):
                dve.wait_ge(tok_done, c.k + 1)
                dve.wait_ge(base_in[c.par], 32 * c.pair + 32)
                wait_past(dve, xn1_saved, c.k - 3)
                wait_past(dve, h2_saved, c.k - 3)
                dve.scalar_tensor_tensor(h1[c.quad][:, :, :], ps_tok, 0.1, base[c.par][:, :, :],
                                         ALU.mult, ALU.add).then_inc(h1_saved, 1)

            def second_residual(c):
                dve.wait_ge(attn_done, c.k + 1)
                wait_past(dve, xn2_saved, c.k - 3)
                wait_past(dve, out_saved, 2 * c.k - 6)
                dve.tensor_tensor(h2[c.quad][:, :, :], ps_attn, h1[c.quad][:, :, :], ALU.add)\
                   .then_inc(h2_saved, 1)

            def spread_k(c):
                dve.wait_ge(k_saved, c.k + 1)
                for t in range(2):
                    wait_past(dve, scores_done[t], c.k - 1)
                for i in range(4):
                    last = dve.tensor_scalar(k_slots[c.par][:, :, i, :], k_t[c.par][:, :, :],
                                             slot_mask[:, i:i + 1], None, ALU.mult)
                last.then_inc(k_spread, 1)

            def take_max(c, t):
                dve.wait_ge(scores_saved[t], c.k + 1)
                wait_past(dve, scores_shifted[t], c.k)
                dve.tensor_reduce(score_max[t][:, :], scores[t][:, :, :], AX.X, ALU.max)\
                   .then_inc(max_done[t], 1)

            def sums(c, t):
                dve.wait_ge(exp_done[t], c.k + 1)
                wait_past(dve, probs_scaled[t], c.k)
                dve.tensor_reduce(prob_sum[t][:, :], probs[t][:, :, :], AX.X, ALU.add).then_inc(sum_done[t], 1)
                dve.wait_ge(sum_done[t], c.k + 1)
                dve.reciprocal(prob_inv[t][:, :], prob_sum[t][:, :]).then_inc(inv_done[t], 1)

            def turn_probs(c, t):
                dve.wait_ge(probs_scaled[t], c.k + 1)
                wait_past(dve, ctx_done[t], c.k - 1)
                dve.transpose(probs_t[c.par][t][:, :, :], probs_n[t][:, :, :]).then_inc(probs_turned[t], 1)

            def shift_gate(c):
                dve.wait_ge(ffn_done, c.k + 1)
                wait_past(dve, gate_exp_done, c.k - 1)
                dve.tensor_reduce(gate_max[c.par][:, :], ps_ffn[:, :, DIM:], AX.X, ALU.max)\
                   .then_inc(gate_max_done, 1)
                dve.wait_ge(gate_max_done, c.k + 1)
                dve.tensor_tensor(gate_shift[c.par][:, :, :], ps_ffn[:, :, DIM:],
                                  gate_max[c.par][:, :].unsqueeze(2).to_broadcast([128, 2, N_EXP]),
                                  ALU.subtract).then_inc(gate_shifted, 1)

            def best_probability(c):
                dve.wait_ge(gate_exp_done, c.k + 1)
                wait_past(dve, out_saved, 2 * c.k - 2)
                dve.tensor_reduce(gate_sum[c.par][:, :], gate_exp[c.par][:, :, :], AX.X, ALU.add)\
                   .then_inc(gate_sum_done, 1)
                dve.wait_ge(gate_sum_done, c.k + 1)
                dve.reciprocal(gate_best[c.par][:, :], gate_sum[c.par][:, :]).then_inc(gate_ready, 1)

            def final_residual(c):
                dve.wait_ge(gate_ready, c.k + 1)
                wait_past(dve, out_stored[c.par], 16 * c.pair)
                for t in range(2):
                    dve.scalar_tensor_tensor(out_sb[c.par][:, t, :], ps_ffn[:, t, 0:DIM],
                                             gate_best[c.par][:, t:t + 1], h2[c.quad][:, t, :],
                                             ALU.mult, ALU.add).then_inc(out_saved, 1)

            def step(chunk_of):
                if (c := chunk_of(1)) is not None:
                    statistics(0, c, h1[c.quad])
                    if is_first(c):
                        split_weights(("wq", "wk", "wv"), (wq_sb, wk_sb, wv_sb), 0)
                if (c := chunk_of(5)) is not None:
                    best_probability(c)
                if (c := chunk_of(3)) is not None:
                    save_lo(c, ps_ctx, ctx_hi, ctx_lo, ctx_hi_saved, ctx_lo_saved, attn_done)
                if (c := chunk_of(5)) is not None:
                    final_residual(c)
                if (c := chunk_of(2)) is not None:
                    take_max(c, 1)
                if (c := chunk_of(4)) is not None:
                    save_lo(c, ps_xn2_t, xn2_hi, xn2_lo, xn2_hi_saved, xn2_lo_saved, ffn_done)
                if (c := chunk_of(2)) is not None:
                    take_max(c, 0)
                if (c := chunk_of(3)) is not None:
                    second_residual(c)
                    statistics(1, c, h2[c.quad])
                if (c := chunk_of(0)) is not None:
                    mask_experts(c)
                if (c := chunk_of(2)) is not None:
                    sums(c, 1)
                if (c := chunk_of(1)) is not None:
                    save_lo(c, ps_xn1_t, xn1_hi, xn1_lo, xn1_hi_saved, xn1_lo_saved, v_done)
                if (c := chunk_of(2)) is not None:
                    sums(c, 0)
                    turn_probs(c, 1)
                if (c := chunk_of(4)) is not None:
                    shift_gate(c)
                if (c := chunk_of(1)) is not None:
                    spread_k(c)
                    if is_first(c):
                        split_weights(("wo", "wf"), (wo_sb, wf_sb), 3)
                        split_biases()
                if (c := chunk_of(2)) is not None:
                    turn_probs(c, 0)
                if (c := chunk_of(0)) is not None:
                    first_residual(c)

            run_steps(dve, step)

        @block.tensor
        def _(pe):
            def turn(src, dst, sem_done):
                for a in range(HALVES):
                    for t in range(2):
                        last = pe.transpose(dst[:, a, t * TILE:(t + 1) * TILE],
                                            src[:, t, a * 128:(a + 1) * 128], ident)
                last.then_inc(sem_done, 1)

            def features_out(dst, weight, src_hi, src_lo, sem_done):
                w_hi, w_lo = weight
                passes = ((w_hi, src_hi), (w_hi, src_lo), (w_lo, src_hi))
                for m in range(HALVES):
                    for a in range(HALVES):
                        for n, (w, src) in enumerate(passes):
                            last = pe.matmul(dst[:, m, :], w[:, a, m * 128:(m + 1) * 128], src[:, a, :],
                                             start=(a == 0 and n == 0), stop=(a == HALVES - 1 and n == 2))
                last.then_inc(sem_done, 1)

            def tokens_out(dst, weight, src_hi, src_lo, sem_done, bias=None):
                w_hi, w_lo = weight
                passes = ((src_hi, w_hi), (src_hi, w_lo), (src_lo, w_hi))
                for t in range(2):
                    for a in range(HALVES):
                        for n, (src, w) in enumerate(passes):
                            last = pe.matmul(dst[:, t, :], src[:, a, t * TILE:(t + 1) * TILE], w[:, a, :],
                                             start=(a == 0 and n == 0),
                                             stop=(a == HALVES - 1 and n == 2 and bias is None))
                    if bias is not None:
                        last = pe.matmul(dst[:, t, :], ones_bf[:, :], bias, start=False, stop=True)
                last.then_inc(sem_done, 1)

            def turn_base(c):
                if is_first(c):
                    pe.wait_ge(s_consts, 16)
                pe.wait_ge(base_in[c.par], 32 * c.pair + 32)
                wait_past(pe, base_t_saved, c.k)
                wait_past(pe, h1_saved, c.k)
                turn(base[c.par], ps_base_t, base_turned)

            def spread_domains(c):
                if is_first(c):
                    pe.wait_ge(s_setup_v, 1)
                pe.wait_ge(dom_cast, c.k + 1)
                wait_past(pe, dom_saved, c.k)
                wait_past(pe, ctx_lo_saved, c.k - 2)
                for t in range(2):
                    last = pe.matmul(ps_dom[:, t * TILE:(t + 1) * TILE],
                                     dom_bf[c.par][:, t:t + 1].to_broadcast([128, 128]), ident_bf[:, :],
                                     start=True, stop=True)
                last.then_inc(dom_spread, 1)

            def expert_product(c):
                if is_first(c):
                    pe.wait_ge(s_wexp, 16)
                pe.wait_ge(base_t_saved, c.k + 1)
                wait_past(pe, expert_masked, c.k)
                for m in range(HALVES):
                    for a in range(HALVES):
                        last = pe.matmul(ps_expert[:, m, :], w_exp_sb[:, a, m * 128:(m + 1) * 128],
                                         base_t[c.par][:, a, :], start=(a == 0), stop=(a == HALVES - 1))
                last.then_inc(expert_done, 1)

            def token_projection(c):
                if is_first(c):
                    pe.wait_ge(s_wproj, 16)
                pe.wait_ge(expert_masked, c.k + 1)
                pe.wait_ge(base_t_saved, c.k + 1)
                wait_past(pe, h1_saved, c.k)
                for t in range(2):
                    for a in range(HALVES):
                        last = pe.matmul(ps_tok[:, t, :], expert_t[c.par][:, a, t * TILE:(t + 1) * TILE],
                                         w_proj_sb[:, a, :], start=(a == 0), stop=(a == HALVES - 1))
                last.then_inc(tok_done, 1)

            def turn_xn1(c):
                pe.wait_ge(xn1_saved, c.k + 1)
                wait_past(pe, scores_saved[1], c.k)
                wait_past(pe, v_saved, c.k)
                wait_past(pe, xn1_lo_saved, c.k)
                turn(xn1[c.par], ps_xn1_t, xn1_turned)

            def kqv_products(c):
                if is_first(c):
                    pe.wait_ge(weights_lo, 3)
                pe.wait_ge(xn1_lo_saved, c.k + 1)
                wait_past(pe, k_saved, c.k)
                wait_past(pe, xn2_lo_saved, c.k - 2)
                features_out(ps_k, parts_of["wk"], xn1_hi[c.par], xn1_lo[c.par], k_done)
                wait_past(pe, q_saved, c.k)
                wait_past(pe, scores_saved[0], c.k)
                features_out(ps_q, parts_of["wq"], xn1_hi[c.par], xn1_lo[c.par], q_done)
                tokens_out(ps_v, parts_of["wv"], xn1_hi[c.par], xn1_lo[c.par], v_done)

            def score_product(c, t):
                pe.wait_ge(q_saved, c.k + 1)
                pe.wait_ge(k_spread, c.k + 1)
                wait_past(pe, scores_saved[t], c.k)
                if t == 1:
                    pe.wait_ge(v_saved, c.k + 1)
                pe.matmul(ps_scores[t], ident_bf[:, :], mask_bf[:, :, :], start=True, stop=False)
                for b in range(BLOCKS):
                    cols = slice(t * TILE + b * BLOCK, t * TILE + (b + 1) * BLOCK)
                    for u in range(4):
                        rows = slice(64 * (u % 2), 64 * (u % 2) + 64)
                        last = pe.matmul(ps_scores[t][32 * u:32 * u + 32, 4 * b:4 * b + 4, :],
                                         q_t[c.par][rows, u // 2, cols],
                                         k_slots[c.par][rows, u // 2, :, cols],
                                         start=False, stop=(b == BLOCKS - 1))
                last.then_inc(scores_done[t], 1)

            def context_product(c, t):
                pe.wait_ge(v_saved, c.k + 1)
                pe.wait_ge(probs_turned[t], c.k + 1)
                wait_past(pe, ctx_lo_saved, c.k)
                pe.wait_ge(dom_saved, at_most_all(c.k + 3))
                for b in range(BLOCKS):
                    for i in range(4):
                        last = pe.matmul(
                            ps_ctx[64 * (i % 2):64 * (i % 2) + 64, i // 2,
                                   t * TILE + b * BLOCK:t * TILE + (b + 1) * BLOCK],
                            v_diag[c.par][:, t, b, i::4],
                            probs_t[c.par][t][:, 4 * b + i, :], start=True, stop=True)
                last.then_inc(ctx_done[t], 1)

            def output_product(c):
                if is_first(c):
                    pe.wait_ge(weights_lo, 4)
                    pe.wait_ge(s_setup_v, 9)
                pe.wait_ge(ctx_lo_saved, c.k + 1)
                wait_past(pe, h2_saved, c.k)
                wait_past(pe, out_saved, 2 * c.k - 2)
                tokens_out(ps_attn, parts_of["wo"], ctx_hi[c.par], ctx_lo[c.par], attn_done,
                           bias_parts[:, 0:DIM])

            def turn_xn2(c):
                pe.wait_ge(xn2_saved, c.k + 1)
                wait_past(pe, xn2_lo_saved, c.k)
                pe.wait_ge(k_saved, at_most_all(c.k + 3))
                turn(xn2[c.par], ps_xn2_t, xn2_turned)

            def feed_forward(c):
                if is_first(c):
                    pe.wait_ge(weights_lo, 5)
                pe.wait_ge(xn2_lo_saved, c.k + 1)
                wait_past(pe, out_saved, 2 * c.k)
                pe.wait_ge(h2_saved, at_most_all(c.k + 2))
                tokens_out(ps_ffn, parts_of["wf"], xn2_hi[c.par], xn2_lo[c.par], ffn_done,
                           bias_parts[:, DIM:])

            def step(chunk_of):
                if (c := chunk_of(3)) is not None:
                    context_product(c, 0)
                if (c := chunk_of(2)) is not None:
                    score_product(c, 1)
                    score_product(c, 0)
                if (c := chunk_of(0)) is not None:
                    turn_base(c)
                    spread_domains(c)
                if (c := chunk_of(3)) is not None:
                    output_product(c)
                if (c := chunk_of(0)) is not None:
                    expert_product(c)
                if (c := chunk_of(4)) is not None:
                    feed_forward(c)
                if (c := chunk_of(1)) is not None:
                    turn_xn1(c)
                if (c := chunk_of(0)) is not None:
                    token_projection(c)
                    if is_first(c):
                        pe.wait_ge(s_columns, 16)
                        pe.wait_ge(s_wof, 16 * 3)
                        for a in range(HALVES):
                            last = pe.matmul(ps_wo_bv, bv_sb[:, a:a + 1], wo_sb[:, a, :],
                                             start=(a == 0), stop=(a == HALVES - 1))
                        last.then_inc(s_setup_p, 1)
                if (c := chunk_of(1)) is not None:
                    kqv_products(c)
                if (c := chunk_of(2)) is not None:
                    context_product(c, 1)
                if (c := chunk_of(3)) is not None:
                    turn_xn2(c)

            run_steps(pe, step)


def lay_out_constants():
    import numpy as np
    c = np.zeros((128, C_END), np.float32)
    p = np.arange(128)
    c[:, C_IDENT:C_IDENT + 128] = np.eye(128)
    query, key = (p % BLOCK)[:, None], np.arange(BLOCK)[None, :]
    seen = (query // 16 == key // 16) & (key <= query)
    c[:, C_MASK:C_MASK + BLOCK] = np.where(seen, 0.0, -1e30)
    c[:, C_SLOT:C_SLOT + 4] = (p // D_HEAD % 4)[:, None] == np.arange(4)[None, :]
    c[:, C_DOMAIN:C_DOMAIN + 2] = (p[:, None] + 128 * np.arange(2)[None, :]) // EXPAND
    return c


def kernel(**inputs):
    import numpy as np
    import concourse.bacc as bacc
    from concourse.bass_utils import run_bass_kernel_spmd

    a = {k: np.asarray(v) for k, v in inputs.items()}
    order = a["x"].reshape(SEQ // DILATION, DILATION, BATCH).transpose(2, 1, 0).reshape(N_CHUNK, 2, 128)
    in_ctx_order = a["L0_attn_Wo"].T.reshape(4, 4, D_HEAD, DIM).transpose(1, 0, 2, 3).reshape(DIM, DIM)
    bv_in_ctx_order = a["L0_attn_bv"].reshape(4, 4, D_HEAD).transpose(1, 0, 2).reshape(DIM)
    wv_in_quad_order = a["L0_attn_Wv"].T.reshape(DIM, 4, 4, D_HEAD).transpose(0, 1, 3, 2).reshape(DIM, DIM)
    per_feature = [a["L0_attn_bq"], a["L0_attn_bk"], bv_in_ctx_order, np.repeat(a["L0_attn_beta"], D_HEAD)]
    arrays = {
        "ids": order.transpose(0, 2, 1).reshape(N_CHUNK * 128, 2),
        "domain_map": a["L0_tok_domain_map"].reshape(VOCAB, 1),
        "emb_table": a["L0_tok_emb_table"],
        "w_exp": a["L0_tok_W_exp"].reshape(DIM, DIM).T,
        "w_proj": a["L0_tok_W_proj"].transpose(0, 2, 1).reshape(DIM, DIM),
        "wq": a["L0_attn_Wq"].T, "wk": a["L0_attn_Wk"].T, "wv": wv_in_quad_order, "wo": in_ctx_order,
        "columns": np.stack([x.reshape(HALVES, 128).T for x in per_feature], 1),
        "bo": a["L0_attn_bo"],
        "wg": a["L0_ffn_Wg"], "bg": a["L0_ffn_bg"], "we": a["L0_ffn_We"], "be": a["L0_ffn_be"],
        "consts": lay_out_constants(),
    }
    arrays = {k: np.ascontiguousarray(v) for k, v in arrays.items()}
    nc = bacc.Bacc("TRN2", target_bir_lowering=False, num_devices=1)
    args = {k: nc.dram_tensor(k, v.shape, mybir.dt.from_np(v.dtype), kind="ExternalInput").ap()
            for k, v in arrays.items()}
    out = nc.dram_tensor("out", (TOKENS, DIM), FP32, kind="ExternalOutput").ap()
    build_lm_tower(nc, out=out, **args)
    r = run_bass_kernel_spmd(nc, [arrays], core_ids=[0])
    got = np.asarray(r.results[0]["out"])
    return got.reshape(BATCH, DILATION, SEQ // DILATION, DIM).transpose(2, 1, 0, 3).reshape(SEQ, BATCH, DIM)
```

```python
import concourse.bass as bass
from concourse import mybir
from contextlib import ExitStack

FP32 = mybir.dt.float32
BF16 = mybir.dt.bfloat16
FP32R = mybir.dt.float32r
INT32 = mybir.dt.int32
ALU = mybir.AluOpType
ACT = mybir.ActivationFunctionType
AX = mybir.AxisListType

SEQ, BATCH = 64, 128
DIM = 256
VOCAB = 50257
N_DOM, EXPAND = 8, 32
HEADS, D_HEAD = 16, 16
DILATION = 4
N_EXP = 8
LN_EPS = 1e-5

TOKENS = SEQ * BATCH
TILE = 128
CHUNK = 2 * TILE
N_CHUNK = TOKENS // CHUNK
BLOCK = 32
BLOCKS = TILE // BLOCK
HALVES = DIM // 128

C_IDENT, C_MASK, C_SLOT, C_DOMAIN, C_END = 0, 128, 160, 164, 166


class Chunk:

    def __init__(self, offset, j=None):
        self.par = offset % 2
        self.quad = offset % 4
        self.k = offset if j is None else 4 * j + offset
        self.pair = offset // 2 if j is None else 2 * j + offset // 2


IDS_LAG, LAST_LAG = -2, 5
LOOP_FROM, LOOP_TO = 10, 30


def run_steps(engine, step):

    def peeled(n):
        step(lambda lag: Chunk(n - lag) if 0 <= n - lag < N_CHUNK else None)

    for n in range(LOOP_FROM):
        peeled(n)
    with engine.Fori(0, (LOOP_TO - LOOP_FROM) // 4) as j:
        for s in range(4):
            step(lambda lag: Chunk(LOOP_FROM + s - lag, j))
    for n in range(LOOP_TO, N_CHUNK + LAST_LAG):
        peeled(n)


def is_first(c):
    return isinstance(c.k, int) and c.k == 0


def wait_past(engine, sem, count):
    if not isinstance(count, int) or count > 0:
        engine.wait_ge(sem, count)


def at_most_all(count):
    return min(count, N_CHUNK) if isinstance(count, int) else count


def build_lm_tower(nc, ids, domain_map, emb_table, w_exp, w_proj, wq, wk, wv, wo, bo, wg, bg, we, be,
                   columns, consts, out):
    ctx = ExitStack()
    with ctx:
        def sb(name, shape, dt=FP32):
            return ctx.enter_context(nc.sbuf_tensor(name, shape, dt))

        def sem(name):
            return ctx.enter_context(nc.semaphore(name))

        const_sb = sb("const_sb", [128, C_END])
        ident = const_sb[:, C_IDENT:C_IDENT + 128]
        causal = const_sb[:, C_MASK:C_MASK + BLOCK]
        slot_mask = const_sb[:, C_SLOT:C_SLOT + 4]
        row_domain = const_sb[:, C_DOMAIN:C_DOMAIN + 2]
        ident_bf = sb("ident_bf", [128, 128], BF16)
        ones_bf = sb("ones_bf", [128, 128], BF16)
        w_exp_sb = sb("w_exp_sb", [128, HALVES, DIM])
        w_proj_sb = sb("w_proj_sb", [128, HALVES, DIM])
        wq_sb = sb("wq_sb", [128, HALVES, DIM])
        wk_sb = sb("wk_sb", [128, HALVES, DIM])
        wv_sb = sb("wv_sb", [128, HALVES, DIM])
        wo_sb = sb("wo_sb", [128, HALVES, DIM])
        wf_sb = sb("wf_sb", [128, HALVES, DIM + N_EXP])
        columns_sb = sb("columns_sb", [128, 4, HALVES])
        bq_sb, bk_sb, bv_sb, beta_sb = (columns_sb[:, n, :] for n in range(4))
        q_scale = sb("q_scale", [128, HALVES])
        q_bias = sb("q_bias", [128, HALVES])
        N_BIAS = 2 * DIM + N_EXP
        parts_of = {name: [sb(f"{name}_{part}", [128, HALVES, width], FP32R) for part in ("hi", "lo")]
                    for name, width in (("w_exp", DIM), ("w_proj", DIM), ("wq", DIM), ("wk", DIM), ("wv", DIM),
                                        ("wo", DIM), ("wf", DIM + N_EXP))}
        bias_row = sb("bias_row", [1, N_BIAS])
        bias_rest = sb("bias_rest", [1, N_BIAS])
        bias_rest2 = sb("bias_rest2", [1, N_BIAS])
        bo_sb = sb("bo_sb", [128, DIM])
        bias_parts = sb("bias_parts", [128, N_BIAS], BF16)
        minus_half = sb("minus_half", [128, 2])
        minus_one = sb("minus_one", [128, 2])
        one = sb("one", [128, 2])
        eps = sb("eps", [128, 2])

        def pair(name, shape, dt=FP32):
            return [sb(f"{name}{p}", shape, dt) for p in range(2)]

        def four(name, shape, dt=FP32):
            return [sb(f"{name}{p}", shape, dt) for p in range(4)]

        id_sb = pair("id_sb", [128, 2], INT32)
        dom_int = pair("dom_int", [128, 2], INT32)
        dom_bf = pair("dom_bf", [128, 2], BF16)
        base = pair("base", [128, 2, DIM])
        base_hi = pair("base_hi", [128, HALVES, CHUNK], FP32R)
        base_lo = pair("base_lo", [128, HALVES, CHUNK], FP32R)
        dom_row = pair("dom_row", [128, CHUNK])
        expert_t = pair("expert_t", [128, HALVES, CHUNK])
        expert_hi = pair("expert_hi", [128, HALVES, CHUNK], FP32R)
        expert_lo = pair("expert_lo", [128, HALVES, CHUNK], FP32R)
        h1 = four("h1", [128, 2, DIM])
        h1_bo = four("h1_bo", [128, 2, DIM])
        xn1 = pair("xn1", [128, 2, DIM])
        xn1_hi = pair("xn1_hi", [128, HALVES, CHUNK], FP32R)
        xn1_lo = pair("xn1_lo", [128, HALVES, CHUNK], FP32R)
        q_t = pair("q_t", [128, HALVES, CHUNK])
        k_t = pair("k_t", [128, HALVES, CHUNK])
        k_slots = pair("k_slots", [128, HALVES, 4, CHUNK])
        v_diag = pair("v_diag", [128, 2, BLOCKS, 4, D_HEAD + 1, 4])
        scores = pair("scores", [128, 16, BLOCK])
        shifted = pair("shifted", [128, 16, BLOCK])
        probs = pair("probs", [128, 16, BLOCK])
        probs_t = [[sb(f"probs_t{p}{t}", [128, 16, BLOCK]) for t in range(2)] for p in range(2)]
        score_max = pair("score_max", [128, 16])
        prob_inv = pair("prob_inv", [128, 2, HEADS])
        context = pair("context", [128, 2, HEADS, D_HEAD])
        ctx_hi = pair("ctx_hi", [128, HALVES, CHUNK], FP32R)
        ctx_lo = pair("ctx_lo", [128, HALVES, CHUNK], FP32R)
        h2 = four("h2", [128, 2, DIM])
        xn2 = pair("xn2", [128, 2, DIM])
        xn2_hi = pair("xn2_hi", [128, HALVES, CHUNK], FP32R)
        xn2_lo = pair("xn2_lo", [128, HALVES, CHUNK], FP32R)
        out_sb = pair("out_sb", [128, 2, DIM])
        gate_max = pair("gate_max", [128, 2])
        gate_shift = pair("gate_shift", [128, 2, N_EXP])
        gate_exp = pair("gate_exp", [128, 2, N_EXP])
        gate_sum = pair("gate_sum", [128, 2])
        gate_best = pair("gate_best", [128, 2])
        ln = []
        for w in (1, 2):
            ln.append(dict(
                raw=pair(f"ln{w}_raw", [128, 2, 6]), stat=pair(f"ln{w}_stat", [128, 2, 2]),
                var=pair(f"ln{w}_var", [128, 2]), rstd=pair(f"ln{w}_rstd", [128, 2]),
                mr=pair(f"ln{w}_mr", [128, 2]), shift=pair(f"ln{w}_shift", [128, 2])))

        ps = ctx.enter_context(nc.psum_tensor("ps", [128, 8, 512], FP32))

        def halves(bank):
            return ps[:, bank, :].rearrange("p (a n) -> p a n", a=2)

        ps_ctx = ps[:, 0:2, 0:HEADS * (D_HEAD + 1)].rearrange("p t (m e) -> p t m e", m=HEADS)
        ps_w_sum, ps_wo_bv = ps[0:1, 0, 0:DIM + N_EXP], ps[0:1, 1, 0:DIM]
        ps_bo, ps_bf = ps[:, 0, 0:DIM], ps[:, 1, 0:DIM + N_EXP]
        ps_ctx_t, ps_xn2_t = halves(0), halves(1)
        ps_base_t, ps_attn = halves(2), halves(2)
        ps_k = halves(3)
        ps_scores = [ps[:, bank, :].rearrange("p (m t) -> p m t", t=BLOCK) for bank in (3, 2)]
        ps_ffn = ps[:, 4:6, 0:DIM + N_EXP]
        ps_dom, ps_expert = ps[:, 4, 0:CHUNK], halves(5)
        ps_v = halves(6)
        ps_q, ps_xn1_t, ps_tok = halves(7), halves(7), halves(7)

        s_consts, s_wexp, s_wproj, s_qkvw, s_wof, s_rows, s_columns = (
            sem(n) for n in ("consts_in", "wexp_in", "wproj_in", "qkv_weights_in", "wo_wffn_in", "bias_rows_in",
                             "columns_in"))
        s_passed = sem("passed")
        s_setup_v, s_setup_g, s_setup_a, s_setup_p = (sem(n) for n in ("setup_vector", "setup_pool", "setup_act",
                                                                       "setup_pe"))
        v_diag_cleared, weights_hi, weights_lo = (sem(n) for n in ("v_diag_cleared", "weights_hi", "weights_lo"))
        ids_in, base_in, dom_in, out_stored = ([sem(f"{n}{p}") for p in range(2)]
                                               for n in ("ids_in", "base_in", "dom_in", "out_stored"))
        dom_cast = sem("dom_cast")
        base_turned, dom_spread, expert_done, tok_done, xn1_turned = (
            sem(n) for n in ("base_turned", "dom_spread", "expert_done", "tok_done", "xn1_turned"))
        q_done, k_done, v_done, ctx_done, ctx_turned, attn_done, xn2_turned, ffn_done = (
            sem(n) for n in ("q_done", "k_done", "v_done", "ctx_done", "ctx_turned", "attn_done", "xn2_turned",
                             "ffn_done"))
        scores_done, scores_masked, max_done, scores_shifted, exp_done, probs_turned = (
                [sem(f"{n}{t}") for t in range(2)]
                for n in ("scores_done", "scores_masked", "max_done", "scores_shifted", "exp_done",
                          "probs_turned"))
        base_hi_saved, dom_saved, expert_hi_saved, xn1_saved, xn1_hi_saved, k_saved, q_saved, v_saved = (
            sem(n) for n in ("base_hi_saved", "dom_saved", "expert_hi_saved", "xn1_saved", "xn1_hi_saved",
                             "k_saved", "q_saved", "v_saved"))
        ctx_hi_saved, xn2_saved, xn2_hi_saved, gate_exp_done = (
            sem(n) for n in ("ctx_hi_saved", "xn2_saved", "xn2_hi_saved", "gate_exp_done"))
        base_lo_saved, expert_masked, h1_saved, xn1_lo_saved, k_spread, inv_done, ctx_saved, ctx_lo_saved = (
            sem(n) for n in ("base_lo_saved", "expert_masked", "h1_saved", "xn1_lo_saved", "k_spread",
                             "inv_done", "ctx_saved", "ctx_lo_saved"))
        h2_saved, xn2_lo_saved, gate_max_done, gate_shifted, gate_sum_done, gate_ready, out_saved = (
            sem(n) for n in ("h2_saved", "xn2_lo_saved", "gate_max_done", "gate_shifted", "gate_sum_done",
                             "gate_ready", "out_saved"))
        ln_raw = [sem(f"ln{w}_raw_done") for w in (1, 2)]
        ln_stat = [sem(f"ln{w}_stat_done") for w in (1, 2)]
        expert_lo_saved, h1_bo_saved = sem("expert_lo_saved"), sem("h1_bo_saved")
        ln_var = [sem(f"ln{w}_var_done") for w in (1, 2)]
        ln_rstd = [sem(f"ln{w}_rstd_done") for w in (1, 2)]
        ln_mr = [sem(f"ln{w}_mr_done") for w in (1, 2)]
        ln_shift = [sem(f"ln{w}_shift_done") for w in (1, 2)]

        def stand_alone(engine, c):
            if not isinstance(c.k, int):
                engine.sem_inc(s_passed, 1)

        ids_by_chunk = ids.rearrange("(c p) t -> c p t", p=128)
        out_by_chunk = out.rearrange("(c t p) f -> c p t f", t=2, p=128)
        block = ctx.enter_context(nc.Block())

        @block.sync
        def _(sp):
            def load_ids(c):
                wait_past(sp, base_in[c.par], 32 * c.pair)
                wait_past(sp, dom_in[c.par], 32 * c.pair)
                stand_alone(sp, c)
                sp.dma_start(id_sb[c.par][:, :], ids_by_chunk[c.k]).then_inc(ids_in[c.par], 16)

            load_ids(Chunk(0))
            load_ids(Chunk(1))
            sp.dma_start(const_sb[:, :], consts).then_inc(s_consts, 16)
            sp.dma_start(columns_sb[:, :, :], columns).then_inc(s_columns, 16)
            sp.dma_start(w_exp_sb[:, :, :], w_exp.rearrange("(a p) m -> p a m", p=128)).then_inc(s_wexp, 16)
            sp.dma_start(w_proj_sb[:, :, :], w_proj.rearrange("(a p) m -> p a m", p=128)).then_inc(s_wproj, 16)
            sp.wait_ge(base_in[0], 32)
            for w, dst in ((wq, wq_sb), (wk, wk_sb), (wv, wv_sb)):
                sp.dma_start(dst[:, :, :], w.rearrange("(a p) m -> p a m", p=128)).then_inc(s_qkvw, 16)
            sp.dma_start(wo_sb[:, :, :], wo.rearrange("(a p) m -> p a m", p=128)).then_inc(s_wof, 16)
            sp.dma_start(wf_sb[:, :, 0:DIM], we.rearrange("(a p) m -> p a m", p=128)).then_inc(s_wof, 16)
            sp.dma_start(wf_sb[:, :, DIM:], wg.rearrange("(a p) m -> p a m", p=128)).then_inc(s_wof, 16)
            for b, at, n in ((bo, 0, DIM), (be, DIM, DIM), (bg, 2 * DIM, N_EXP)):
                sp.dma_start(bias_row[0:1, at:at + n], b.rearrange("(a n) -> a n", a=1)).then_inc(s_rows, 16)

            def step(chunk_of):
                if (c := chunk_of(IDS_LAG)) is not None:
                    load_ids(c)
                if (c := chunk_of(LAST_LAG)) is not None:
                    sp.wait_ge(out_saved, 2 * c.k + 2)
                    stand_alone(sp, c)
                    sp.dma_start(out_by_chunk[c.k], out_sb[c.par][:, :, :]).then_inc(out_stored[c.par], 16)

            run_steps(sp, step)
            for p in range(2):
                sp.wait_ge(out_stored[p], 16 * (N_CHUNK // 2))

        @block.gpsimd
        def _(pool):
            def gather(c):
                pool.wait_ge(ids_in[c.par], 16 * c.pair + 16)
                wait_past(pool, h1_saved, c.k - 1)
                wait_past(pool, dom_cast, c.k - 1)
                stand_alone(pool, c)
                for t in range(2):
                    pool.indirect_dma_start(base[c.par][:, t, :], None, emb_table,
                                            bass.IndirectOffsetOnAxis(id_sb[c.par][:, t:t + 1], 0))\
                        .then_inc(base_in[c.par], 16)
                for t in range(2):
                    pool.indirect_dma_start(dom_int[c.par][:, t:t + 1], None, domain_map,
                                            bass.IndirectOffsetOnAxis(id_sb[c.par][:, t:t + 1], 0))\
                        .then_inc(dom_in[c.par], 16)

            def cast_domains(c):
                pool.wait_ge(dom_in[c.par], 32 * c.pair + 32)
                wait_past(pool, dom_spread, c.k - 1)
                stand_alone(pool, c)
                pool.tensor_copy(dom_bf[c.par][:, :], dom_int[c.par][:, :]).then_inc(dom_cast, 1)

            def layernorm_scalars(w, c):
                L, p = ln[w], c.par
                pool.wait_ge(ln_stat[w], c.k + 1)
                wait_past(pool, xn1_saved if w == 0 else xn2_saved, c.k - 1)
                pool.tensor_tensor(L["var"][p][:, :], L["stat"][p][:, :, 1], eps[:, :], ALU.add)\
                    .then_inc(ln_var[w], 1)
                pool.wait_ge(ln_var[w], c.k + 1)
                pool.tensor_tensor(L["rstd"][p][:, :], L["var"][p][:, :], minus_half[:, :], ALU.pow)\
                    .then_inc(ln_rstd[w], 1)
                pool.wait_ge(ln_rstd[w], c.k + 1)
                pool.tensor_tensor(L["mr"][p][:, :], L["stat"][p][:, :, 0], L["rstd"][p][:, :], ALU.mult)\
                    .then_inc(ln_mr[w], 1)
                pool.wait_ge(ln_mr[w], c.k + 1)
                if w == 0:
                    pool.tensor_tensor(L["shift"][p][:, :], L["mr"][p][:, :], minus_one[:, :], ALU.mult)\
                        .then_inc(ln_shift[w], 1)
                else:
                    pool.tensor_tensor(L["shift"][p][:, :], one[:, :], L["mr"][p][:, :], ALU.subtract)\
                        .then_inc(ln_shift[w], 1)

            def save_expert_lo(c):
                pool.wait_ge(expert_hi_saved, c.k + 1)
                wait_past(pool, tok_done, c.k - 1)
                pool.tensor_tensor(expert_lo[c.par][:, :, :], expert_t[c.par][:, :, :],
                                   expert_hi[c.par][:, :, :].bitcast(FP32), ALU.subtract)\
                    .then_inc(expert_lo_saved, 1)

            def add_output_bias(c):
                pool.wait_ge(h1_saved, c.k + 1)
                if is_first(c):
                    pool.wait_ge(s_setup_a, 2)
                wait_past(pool, h2_saved, c.k - 3)
                pool.tensor_tensor(h1_bo[c.quad][:, :, :], h1[c.quad][:, :, :],
                                   bo_sb[:, :].unsqueeze(1).to_broadcast([128, 2, DIM]), ALU.add)\
                    .then_inc(h1_bo_saved, 1)

            def shift_scores(c, t):
                pool.wait_ge(max_done[t], c.k + 1)
                wait_past(pool, exp_done[t], c.k)
                pool.tensor_tensor(shifted[t][:, :, :], scores[t][:, :, :],
                                   score_max[t][:, :].unsqueeze(2).to_broadcast([128, 16, BLOCK]),
                                   ALU.subtract).then_inc(scores_shifted[t], 1)

            for tile, value in ((minus_half, -0.5), (minus_one, -1.0), (one, 1.0), (eps, LN_EPS)):
                pool.memset(tile[:, :], value).then_inc(s_setup_g, 1)
            pool.wait_ge(s_setup_g, 4)

            def step(chunk_of):
                if (c := chunk_of(4)) is not None:
                    shift_scores(c, 0)
                if (c := chunk_of(1)) is not None:
                    cast_domains(c)
                if (c := chunk_of(4)) is not None:
                    add_output_bias(c)
                    shift_scores(c, 1)
                if (c := chunk_of(2)) is not None:
                    layernorm_scalars(0, c)
                if (c := chunk_of(0)) is not None:
                    gather(c)
                if (c := chunk_of(1)) is not None:
                    save_expert_lo(c)
                if (c := chunk_of(5)) is not None:
                    layernorm_scalars(1, c)

            run_steps(pool, step)

        @block.scalar
        def _(act):
            act.wait_ge(s_columns, 16)
            act.activation(q_scale[:, :], beta_sb[:, :], ACT.Exp, scale=-1.0).then_inc(s_setup_a, 1)

            def round_weights(names, sbs, arrived, count):
                act.wait_ge(arrived, count)
                for name, w_sb in zip(names, sbs):
                    act.activation(parts_of[name][0][:, :, :], w_sb[:, :, :], ACT.Copy).then_inc(weights_hi, 1)

            round_weights(("w_exp",), (w_exp_sb,), s_wexp, 16)
            round_weights(("w_proj",), (w_proj_sb,), s_wproj, 16)

            def save_domains(c):
                act.wait_ge(dom_spread, c.k + 1)
                wait_past(act, expert_masked, c.k - 1)
                act.activation(dom_row[c.par][:, :], ps_dom, ACT.Copy).then_inc(dom_saved, 1)

            def normalise(w, c, src, dst, saved, turned):
                L, p = ln[w], c.par
                act.wait_ge(ln_shift[w], c.k + 1)
                wait_past(act, turned, c.k - 1)
                for t in range(2):
                    last = act.activation(dst[p][:, t, :], src[:, t, :], ACT.Identity,
                                          scale=L["rstd"][p][:, t:t + 1], bias=L["shift"][p][:, t:t + 1])
                last.then_inc(saved, 1)

            def save_hi(c, psum, hi, produced, saved, used):
                act.wait_ge(produced, c.k + 1)
                wait_past(act, used, c.k - 1)
                act.activation(hi[c.par][:, :, :], psum, ACT.Copy).then_inc(saved, 1)

            def save_expert_hi(c):
                act.wait_ge(expert_masked, c.k + 1)
                wait_past(act, tok_done, c.k - 1)
                act.activation(expert_hi[c.par][:, :, :], expert_t[c.par][:, :, :], ACT.Copy)\
                   .then_inc(expert_hi_saved, 1)

            def save_output_bias():
                act.wait_ge(s_setup_p, 2)
                act.activation(bo_sb[:, :], ps_bo, ACT.Copy).then_inc(s_setup_a, 1)

            def gate_exponentials(c):
                act.wait_ge(gate_shifted, c.k + 1)
                wait_past(act, gate_sum_done, c.k - 1)
                act.activation(gate_exp[c.par][:, :, :], gate_shift[c.par][:, :, :], ACT.Exp)\
                   .then_inc(gate_exp_done, 1)

            def save_k(c):
                act.wait_ge(k_done, c.k + 1)
                wait_past(act, k_spread, c.k - 1)
                for a in range(HALVES):
                    last = act.activation(k_t[c.par][:, a, :], ps_k[:, a, :], ACT.Identity,
                                          bias=bk_sb[:, a:a + 1])
                last.then_inc(k_saved, 1)

            def save_q(c):
                act.wait_ge(q_done, c.k + 1)
                if is_first(c):
                    act.wait_ge(s_setup_v, 3)
                for t in range(2):
                    wait_past(act, scores_done[t], c.k - 1)
                for a in range(HALVES):
                    last = act.activation(q_t[c.par][:, a, :], ps_q[:, a, :], ACT.Identity,
                                          scale=q_scale[:, a:a + 1], bias=q_bias[:, a:a + 1])
                last.then_inc(q_saved, 1)

            def save_v_diagonal(c):
                act.wait_ge(v_done, c.k + 1)
                wait_past(act, ctx_done, c.k - 1)
                if isinstance(c.k, int) and c.k < 2:
                    act.wait_ge(v_diag_cleared, 2 * c.k + 2)
                for b in range(BLOCKS):
                    for u in range(4):
                        last = act.activation(v_diag[c.par][32 * u:32 * u + 32, :, b, u, 0:D_HEAD, :],
                                              ps_v[32 * b:32 * b + 32, :, 64 * u:64 * u + 64]
                                              .rearrange("p t (d i) -> p t d i", i=4), ACT.Copy)
                last.then_inc(v_saved, 1)

            def exponentials(c, t):
                act.wait_ge(scores_shifted[t], c.k + 1)
                wait_past(act, probs_turned[t], c.k)
                act.activation(probs[t][:, :, :], shifted[t][:, :, :], ACT.Exp).then_inc(exp_done[t], 1)

            def step(chunk_of):
                if (c := chunk_of(5)) is not None:
                    normalise(1, c, h2[c.quad], xn2, xn2_saved, xn2_turned)
                if (c := chunk_of(2)) is not None:
                    save_k(c)
                if (c := chunk_of(0)) is not None:
                    save_hi(c, ps_base_t, base_hi, base_turned, base_hi_saved, expert_done)
                if (c := chunk_of(4)) is not None:
                    save_hi(c, ps_ctx_t, ctx_hi, ctx_turned, ctx_hi_saved, attn_done)
                if (c := chunk_of(0)) is not None:
                    save_domains(c)
                    if is_first(c):
                        round_weights(("wq", "wk", "wv"), (wq_sb, wk_sb, wv_sb), s_qkvw, 16 * 3)
                if (c := chunk_of(5)) is not None:
                    save_hi(c, ps_xn2_t, xn2_hi, xn2_turned, xn2_hi_saved, ffn_done)
                if (c := chunk_of(3)) is not None:
                    exponentials(c, 0)
                    exponentials(c, 1)
                if (c := chunk_of(2)) is not None:
                    save_q(c)
                if (c := chunk_of(1)) is not None:
                    normalise(0, c, h1[c.quad], xn1, xn1_saved, xn1_turned)
                if (c := chunk_of(0)) is not None:
                    save_expert_hi(c)
                if (c := chunk_of(1)) is not None:
                    save_hi(c, ps_xn1_t, xn1_hi, xn1_turned, xn1_hi_saved, v_done)
                if (c := chunk_of(2)) is not None:
                    save_v_diagonal(c)
                if (c := chunk_of(5)) is not None:
                    gate_exponentials(c)
                if (c := chunk_of(1)) is not None:
                    if is_first(c):
                        round_weights(("wo",), (wo_sb,), s_wof, 16 * 3)
                        save_output_bias()
                if (c := chunk_of(2)) is not None:
                    if is_first(c):
                        round_weights(("wf",), (wf_sb,), s_setup_v, 10)

            run_steps(act, step)

        @block.vector
        def _(dve):
            dve.wait_ge(s_consts, 16)
            dve.tensor_copy(ident_bf[:, :], ident)
            dve.memset(ones_bf[:, :], 1.0)
            dve.memset(bias_parts[:, :], 0.0).then_inc(s_setup_v, 1)
            dve.wait_ge(s_setup_a, 1)
            dve.tensor_scalar(q_scale[:, :], q_scale[:, :], float(D_HEAD) ** -0.5, None, ALU.mult)\
               .then_inc(s_setup_v, 1)
            dve.wait_ge(s_setup_v, 2)
            dve.tensor_tensor(q_bias[:, :], bq_sb[:, :], q_scale[:, :], ALU.mult).then_inc(s_setup_v, 1)
            def split_biases():
                dve.wait_ge(s_setup_p, 1)
                dve.wait_ge(s_rows, 16 * 3)
                dve.tensor_tensor(bias_row[0:1, 0:DIM], ps_wo_bv, bias_row[0:1, 0:DIM], ALU.add)
                dve.tensor_tensor(bias_row[0:1, DIM:], ps_w_sum, bias_row[0:1, DIM:], ALU.add)\
                   .then_inc(s_setup_v, 1)
                dve.wait_ge(s_setup_v, 4)
                dve.tensor_copy(bias_parts[0:1, :], bias_row[0:1, :]).then_inc(s_setup_v, 1)
                dve.wait_ge(s_setup_v, 5)
                dve.tensor_tensor(bias_rest[0:1, :], bias_row[0:1, :], bias_parts[0:1, :], ALU.subtract)\
                   .then_inc(s_setup_v, 1)
                dve.wait_ge(s_setup_v, 6)
                dve.tensor_copy(bias_parts[32:33, :], bias_rest[0:1, :])
                dve.tensor_copy(bias_row[0:1, :].bitcast(BF16)[:, 0:N_BIAS], bias_rest[0:1, :])\
                   .then_inc(s_setup_v, 1)
                dve.wait_ge(s_setup_v, 7)
                dve.tensor_tensor(bias_rest2[0:1, :], bias_rest[0:1, :],
                                  bias_row[0:1, :].bitcast(BF16)[:, 0:N_BIAS], ALU.subtract)\
                   .then_inc(s_setup_v, 1)
                dve.wait_ge(s_setup_v, 8)
                dve.tensor_copy(bias_parts[64:65, :], bias_rest2[0:1, :]).then_inc(s_setup_v, 1)

            def fold_feed_forward_bias():
                dve.wait_ge(s_setup_p, 2)
                for a in range(HALVES):
                    last = dve.scalar_tensor_tensor(wf_sb[:, a, :], ps_bf, 1.0 / DIM, wf_sb[:, a, :],
                                                    ALU.mult, ALU.add)
                last.then_inc(s_setup_v, 1)

            def split_weights(names, sbs, done_before):
                for n, (name, w_sb) in enumerate(zip(names, sbs)):
                    hi, lo = parts_of[name]
                    dve.wait_ge(weights_hi, done_before + n + 1)
                    dve.tensor_tensor(lo[:, :, :], w_sb[:, :, :], hi[:, :, :].bitcast(FP32), ALU.subtract)\
                       .then_inc(weights_lo, 1)

            def clear_v_diagonal(p):
                dve.memset(v_diag[p][:, :, :, :, :, :], 0.0).then_inc(v_diag_cleared, 1)
                dve.wait_ge(v_diag_cleared, 2 * p + 1)
                for u in range(4):
                    last = dve.memset(v_diag[p][32 * u:32 * u + 32, :, :, u, D_HEAD, :], 1.0)
                last.then_inc(v_diag_cleared, 1)

            clear_v_diagonal(0)
            split_weights(("w_exp",), (w_exp_sb,), 0)

            def save_lo(c, psum, hi, lo, hi_saved, saved, used):
                dve.wait_ge(hi_saved, c.k + 1)
                wait_past(dve, used, c.k - 1)
                dve.tensor_tensor(lo[c.par][:, :, :], psum, hi[c.par][:, :, :].bitcast(FP32), ALU.subtract)\
                   .then_inc(saved, 1)

            def statistics(w, c, src):
                L, p = ln[w], c.par
                dve.wait_ge(h1_saved if w == 0 else h2_saved, c.k + 1)
                wait_past(dve, ln_shift[w], c.k - 1)
                for t in range(2):
                    last = dve.bn_stats(L["raw"][p][:, t, :], src[:, t, :])
                last.then_inc(ln_raw[w], 1)
                dve.wait_ge(ln_raw[w], c.k + 1)
                stand_alone(dve, c)
                for t in range(2):
                    last = dve.bn_aggr(L["stat"][p][:, t, :], L["raw"][p][:, t, :])
                last.then_inc(ln_stat[w], 1)

            def mask_experts(c):
                dve.wait_ge(expert_done, c.k + 1)
                dve.wait_ge(dom_saved, c.k + 1)
                wait_past(dve, expert_lo_saved, c.k - 1)
                for a in range(HALVES):
                    last = dve.scalar_tensor_tensor(expert_t[c.par][:, a, :], dom_row[c.par][:, :],
                                                    row_domain[:, a:a + 1], ps_expert[:, a, :],
                                                    ALU.is_equal, ALU.mult)
                last.then_inc(expert_masked, 1)

            def first_residual(c):
                dve.wait_ge(tok_done, c.k + 1)
                dve.wait_ge(base_in[c.par], 32 * c.pair + 32)
                wait_past(dve, xn1_saved, c.k - 3)
                wait_past(dve, h1_bo_saved, c.k - 3)
                dve.scalar_tensor_tensor(h1[c.quad][:, :, :], ps_tok, 0.1, base[c.par][:, :, :],
                                         ALU.mult, ALU.add).then_inc(h1_saved, 1)

            def second_residual(c):
                dve.wait_ge(attn_done, c.k + 1)
                dve.wait_ge(h1_bo_saved, c.k + 1)
                wait_past(dve, xn2_saved, c.k - 3)
                wait_past(dve, out_saved, 2 * c.k - 6)
                dve.tensor_tensor(h2[c.quad][:, :, :], ps_attn, h1_bo[c.quad][:, :, :], ALU.add)\
                   .then_inc(h2_saved, 1)

            def spread_k(c):
                dve.wait_ge(k_saved, c.k + 1)
                for t in range(2):
                    wait_past(dve, scores_done[t], c.k - 1)
                for i in range(4):
                    last = dve.tensor_scalar(k_slots[c.par][:, :, i, :], k_t[c.par][:, :, :],
                                             slot_mask[:, i:i + 1], None, ALU.mult)
                last.then_inc(k_spread, 1)

            def mask_scores(c, t):
                dve.wait_ge(scores_done[t], c.k + 1)
                wait_past(dve, scores_shifted[t], c.k)
                dve.tensor_tensor(scores[t][:, :, :], ps_scores[t],
                                  causal.unsqueeze(1).to_broadcast([128, 16, BLOCK]), ALU.add)\
                   .then_inc(scores_masked[t], 1)

            def take_max(c, t):
                dve.wait_ge(scores_masked[t], c.k + 1)
                dve.tensor_reduce(score_max[t][:, :], scores[t][:, :, :], AX.X, ALU.max)\
                   .then_inc(max_done[t], 1)

            def turn_probs(c, t):
                dve.wait_ge(exp_done[t], c.k + 1)
                wait_past(dve, ctx_done, c.k - 1)
                dve.transpose(probs_t[c.par][t][:, :, :], probs[t][:, :, :]).then_inc(probs_turned[t], 1)

            def divide_context(c):
                dve.wait_ge(ctx_done, c.k + 1)
                wait_past(dve, ctx_turned, c.k - 1)
                dve.reciprocal(prob_inv[c.par][:, :, :], ps_ctx[:, :, :, D_HEAD]).then_inc(inv_done, 1)
                dve.wait_ge(inv_done, c.k + 1)
                dve.tensor_tensor(context[c.par][:, :, :, :], ps_ctx[:, :, :, 0:D_HEAD],
                                  prob_inv[c.par][:, :, :].unsqueeze(3).to_broadcast([128, 2, HEADS, D_HEAD]),
                                  ALU.mult).then_inc(ctx_saved, 1)

            def shift_gate(c):
                dve.wait_ge(ffn_done, c.k + 1)
                wait_past(dve, gate_exp_done, c.k - 1)
                dve.tensor_reduce(gate_max[c.par][:, :], ps_ffn[:, :, DIM:], AX.X, ALU.max)\
                   .then_inc(gate_max_done, 1)
                dve.wait_ge(gate_max_done, c.k + 1)
                dve.tensor_tensor(gate_shift[c.par][:, :, :], ps_ffn[:, :, DIM:],
                                  gate_max[c.par][:, :].unsqueeze(2).to_broadcast([128, 2, N_EXP]),
                                  ALU.subtract).then_inc(gate_shifted, 1)

            def best_probability(c):
                dve.wait_ge(gate_exp_done, c.k + 1)
                wait_past(dve, out_saved, 2 * c.k - 2)
                dve.tensor_reduce(gate_sum[c.par][:, :], gate_exp[c.par][:, :, :], AX.X, ALU.add)\
                   .then_inc(gate_sum_done, 1)
                dve.wait_ge(gate_sum_done, c.k + 1)
                dve.reciprocal(gate_best[c.par][:, :], gate_sum[c.par][:, :]).then_inc(gate_ready, 1)

            def final_residual(c):
                dve.wait_ge(gate_ready, c.k + 1)
                wait_past(dve, out_stored[c.par], 16 * c.pair)
                for t in range(2):
                    dve.scalar_tensor_tensor(out_sb[c.par][:, t, :], ps_ffn[:, t, 0:DIM],
                                             gate_best[c.par][:, t:t + 1], h2[c.quad][:, t, :],
                                             ALU.mult, ALU.add).then_inc(out_saved, 1)

            def step(chunk_of):
                if (c := chunk_of(0)) is not None:
                    save_lo(c, ps_base_t, base_hi, base_lo, base_hi_saved, base_lo_saved, expert_done)
                if (c := chunk_of(4)) is not None:
                    save_lo(c, ps_ctx_t, ctx_hi, ctx_lo, ctx_hi_saved, ctx_lo_saved, attn_done)
                if (c := chunk_of(2)) is not None:
                    spread_k(c)
                if (c := chunk_of(3)) is not None:
                    turn_probs(c, 0)
                if (c := chunk_of(5)) is not None:
                    save_lo(c, ps_xn2_t, xn2_hi, xn2_lo, xn2_hi_saved, xn2_lo_saved, ffn_done)
                if (c := chunk_of(3)) is not None:
                    turn_probs(c, 1)
                if (c := chunk_of(0)) is not None:
                    if is_first(c):
                        split_weights(("w_proj",), (w_proj_sb,), 1)
                    mask_experts(c)
                    if is_first(c):
                        split_weights(("wq", "wk", "wv"), (wq_sb, wk_sb, wv_sb), 2)
                        split_biases()
                if (c := chunk_of(4)) is not None:
                    second_residual(c)
                if (c := chunk_of(2)) is not None:
                    mask_scores(c, 0)
                if (c := chunk_of(1)) is not None:
                    save_lo(c, ps_xn1_t, xn1_hi, xn1_lo, xn1_hi_saved, xn1_lo_saved, v_done)
                if (c := chunk_of(4)) is not None:
                    statistics(1, c, h2[c.quad])
                if (c := chunk_of(5)) is not None:
                    shift_gate(c)
                if (c := chunk_of(2)) is not None:
                    take_max(c, 0)
                if (c := chunk_of(5)) is not None:
                    best_probability(c)
                if (c := chunk_of(3)) is not None:
                    divide_context(c)
                if (c := chunk_of(2)) is not None:
                    mask_scores(c, 1)
                    take_max(c, 1)
                if (c := chunk_of(5)) is not None:
                    final_residual(c)
                if (c := chunk_of(0)) is not None:
                    first_residual(c)
                    statistics(0, c, h1[c.quad])
                if (c := chunk_of(1)) is not None:
                    if is_first(c):
                        clear_v_diagonal(1)
                        fold_feed_forward_bias()
                if (c := chunk_of(2)) is not None:
                    if is_first(c):
                        split_weights(("wo",), (wo_sb,), 5)
                if (c := chunk_of(3)) is not None:
                    if is_first(c):
                        split_weights(("wf",), (wf_sb,), 6)

            run_steps(dve, step)

        @block.tensor
        def _(pe):
            def turn(src, dst, sem_done):
                for a in range(HALVES):
                    for t in range(2):
                        last = pe.transpose(dst[:, a, t * TILE:(t + 1) * TILE],
                                            src[:, t, a * 128:(a + 1) * 128], ident)
                last.then_inc(sem_done, 1)

            def features_out(dst, weight, src_hi, src_lo, sem_done):
                w_hi, w_lo = weight
                passes = ((w_hi, src_hi), (w_hi, src_lo), (w_lo, src_hi))
                for m in range(HALVES):
                    for a in range(HALVES):
                        for n, (w, src) in enumerate(passes):
                            last = pe.matmul(dst[:, m, :], w[:, a, m * 128:(m + 1) * 128], src[:, a, :],
                                             start=(a == 0 and n == 0), stop=(a == HALVES - 1 and n == 2))
                last.then_inc(sem_done, 1)

            def tokens_out(dst, weight, src_hi, src_lo, sem_done):
                w_hi, w_lo = weight
                passes = ((src_hi, w_hi), (src_hi, w_lo), (src_lo, w_hi))
                for t in range(2):
                    for a in range(HALVES):
                        for n, (src, w) in enumerate(passes):
                            last = pe.matmul(dst[:, t, :], src[:, a, t * TILE:(t + 1) * TILE], w[:, a, :],
                                             start=(a == 0 and n == 0),
                                             stop=(a == HALVES - 1 and n == 2))
                last.then_inc(sem_done, 1)

            def turn_base(c):
                if is_first(c):
                    pe.wait_ge(s_consts, 16)
                pe.wait_ge(base_in[c.par], 32 * c.pair + 32)
                wait_past(pe, base_lo_saved, c.k)
                wait_past(pe, scores_masked[1], c.k - 2)
                wait_past(pe, h2_saved, c.k - 4)
                turn(base[c.par], ps_base_t, base_turned)

            def spread_domains(c):
                if is_first(c):
                    pe.wait_ge(s_setup_v, 1)
                pe.wait_ge(dom_cast, c.k + 1)
                wait_past(pe, dom_saved, c.k)
                wait_past(pe, out_saved, 2 * c.k - 10)
                for t in range(2):
                    last = pe.matmul(ps_dom[:, t * TILE:(t + 1) * TILE],
                                     dom_bf[c.par][:, t:t + 1].to_broadcast([128, 128]), ident_bf[:, :],
                                     start=True, stop=True)
                last.then_inc(dom_spread, 1)

            def expert_product(c):
                if is_first(c):
                    pe.wait_ge(weights_lo, 1)
                pe.wait_ge(base_lo_saved, c.k + 1)
                wait_past(pe, expert_masked, c.k)
                wait_past(pe, out_saved, 2 * c.k - 10)
                features_out(ps_expert, parts_of["w_exp"], base_hi[c.par], base_lo[c.par], expert_done)

            def token_projection(c):
                if is_first(c):
                    pe.wait_ge(weights_lo, 2)
                pe.wait_ge(expert_lo_saved, c.k + 1)
                wait_past(pe, h1_saved, c.k)
                wait_past(pe, q_saved, c.k - 1)
                wait_past(pe, xn1_lo_saved, c.k)
                tokens_out(ps_tok, parts_of["w_proj"], expert_hi[c.par], expert_lo[c.par], tok_done)

            def turn_xn1(c):
                pe.wait_ge(xn1_saved, c.k + 1)
                wait_past(pe, xn1_lo_saved, c.k)
                wait_past(pe, q_saved, c.k)
                pe.wait_ge(h1_saved, c.k + 1)
                turn(xn1[c.par], ps_xn1_t, xn1_turned)

            def k_product(c):
                if is_first(c):
                    pe.wait_ge(weights_lo, 5)
                pe.wait_ge(xn1_lo_saved, c.k + 1)
                wait_past(pe, k_saved, c.k)
                wait_past(pe, scores_masked[0], c.k)
                features_out(ps_k, parts_of["wk"], xn1_hi[c.par], xn1_lo[c.par], k_done)

            def q_product(c):
                pe.wait_ge(xn1_lo_saved, c.k + 1)
                wait_past(pe, q_saved, c.k)
                pe.wait_ge(h1_saved, at_most_all(c.k + 2))
                features_out(ps_q, parts_of["wq"], xn1_hi[c.par], xn1_lo[c.par], q_done)

            def v_product(c):
                pe.wait_ge(xn1_lo_saved, c.k + 1)
                wait_past(pe, v_saved, c.k)
                tokens_out(ps_v, parts_of["wv"], xn1_hi[c.par], xn1_lo[c.par], v_done)

            def score_product(c, t):
                pe.wait_ge(q_saved, c.k + 1)
                pe.wait_ge(k_spread, c.k + 1)
                wait_past(pe, scores_masked[t], c.k)
                if t == 0:
                    pe.wait_ge(k_saved, c.k + 1)
                else:
                    pe.wait_ge(base_lo_saved, at_most_all(c.k + 3))
                    wait_past(pe, h2_saved, c.k - 1)
                stand_alone(pe, c)
                for b in range(BLOCKS):
                    cols = slice(t * TILE + b * BLOCK, t * TILE + (b + 1) * BLOCK)
                    for u in range(4):
                        rows = slice(64 * (u % 2), 64 * (u % 2) + 64)
                        last = pe.matmul(ps_scores[t][32 * u:32 * u + 32, 4 * b:4 * b + 4, :],
                                         q_t[c.par][rows, u // 2, cols],
                                         k_slots[c.par][rows, u // 2, :, cols], start=True, stop=True)
                last.then_inc(scores_done[t], 1)

            def context_product(c):
                if is_first(c):
                    pe.wait_ge(s_setup_a, 2)
                    pe.wait_ge(s_setup_v, 10)
                pe.wait_ge(v_saved, c.k + 1)
                for t in range(2):
                    pe.wait_ge(probs_turned[t], c.k + 1)
                wait_past(pe, ctx_saved, c.k)
                wait_past(pe, ctx_lo_saved, c.k)
                wait_past(pe, xn2_lo_saved, c.k - 1)
                for t in range(2):
                    for i in range(4):
                        for b in range(BLOCKS):
                            last = pe.matmul(ps_ctx[32 * b:32 * b + 32, t, 4 * i:4 * i + 4, :],
                                             probs_t[c.par][t][:, 4 * b + i, :],
                                             v_diag[c.par][:, t, b, :, :, i], start=True, stop=True)
                last.then_inc(ctx_done, 1)

            def turn_context(c):
                pe.wait_ge(ctx_saved, c.k + 1)
                wait_past(pe, ctx_lo_saved, c.k)
                turn(context[c.par][:, :, :, :].rearrange("p t m d -> p t (m d)"), ps_ctx_t, ctx_turned)

            def output_product(c):
                if is_first(c):
                    pe.wait_ge(weights_lo, 6)
                pe.wait_ge(ctx_lo_saved, c.k + 1)
                wait_past(pe, h2_saved, c.k)
                pe.wait_ge(scores_masked[1], at_most_all(c.k + 2))
                pe.wait_ge(base_lo_saved, at_most_all(c.k + 5))
                tokens_out(ps_attn, parts_of["wo"], ctx_hi[c.par], ctx_lo[c.par], attn_done)

            def turn_xn2(c):
                pe.wait_ge(xn2_saved, c.k + 1)
                wait_past(pe, xn2_lo_saved, c.k)
                pe.wait_ge(ctx_saved, at_most_all(c.k + 2))
                turn(xn2[c.par], ps_xn2_t, xn2_turned)

            def feed_forward(c):
                if is_first(c):
                    pe.wait_ge(weights_lo, 7)
                pe.wait_ge(xn2_lo_saved, c.k + 1)
                wait_past(pe, out_saved, 2 * c.k)
                pe.wait_ge(dom_saved, at_most_all(c.k + 6))
                pe.wait_ge(expert_masked, at_most_all(c.k + 6))
                tokens_out(ps_ffn, parts_of["wf"], xn2_hi[c.par], xn2_lo[c.par], ffn_done)

            def add_up_v_bias():
                pe.wait_ge(s_setup_g, 2)
                pe.wait_ge(s_columns, 16)
                pe.wait_ge(s_wof, 16 * 3)
                for a in range(HALVES):
                    pe.matmul(ps_wo_bv, bv_sb[:, a:a + 1], wo_sb[:, a, :],
                              start=(a == 0), stop=(a == HALVES - 1))
                for a in range(HALVES):
                    last = pe.matmul(ps_w_sum, minus_one[:, 0:1], wf_sb[:, a, :],
                                     start=(a == 0), stop=(a == HALVES - 1))
                last.then_inc(s_setup_p, 1)

            def spread_biases():
                pe.wait_ge(s_setup_v, 9)
                pe.matmul(ps_bo, ones_bf[:, :], bias_parts[:, 0:DIM], start=True, stop=True)
                pe.matmul(ps_bf, ones_bf[:, :], bias_parts[:, DIM:], start=True, stop=True)\
                  .then_inc(s_setup_p, 1)

            def step(chunk_of):
                if (c := chunk_of(2)) is not None:
                    k_product(c)
                if (c := chunk_of(1)) is not None:
                    token_projection(c)
                if (c := chunk_of(4)) is not None:
                    turn_context(c)
                if (c := chunk_of(5)) is not None:
                    turn_xn2(c)
                if (c := chunk_of(0)) is not None:
                    turn_base(c)
                if (c := chunk_of(2)) is not None:
                    v_product(c)
                if (c := chunk_of(0)) is not None:
                    spread_domains(c)
                if (c := chunk_of(2)) is not None:
                    q_product(c)
                if (c := chunk_of(4)) is not None:
                    output_product(c)
                if (c := chunk_of(0)) is not None:
                    expert_product(c)
                if (c := chunk_of(2)) is not None:
                    score_product(c, 0)
                if (c := chunk_of(1)) is not None:
                    turn_xn1(c)
                if (c := chunk_of(5)) is not None:
                    feed_forward(c)
                if (c := chunk_of(3)) is not None:
                    context_product(c)
                if (c := chunk_of(2)) is not None:
                    score_product(c, 1)
                if (c := chunk_of(0)) is not None:
                    if is_first(c):
                        add_up_v_bias()
                if (c := chunk_of(1)) is not None:
                    if is_first(c):
                        spread_biases()

            run_steps(pe, step)


def lay_out_constants():
    import numpy as np
    c = np.zeros((128, C_END), np.float32)
    p = np.arange(128)
    c[:, C_IDENT:C_IDENT + 128] = np.eye(128)
    query, key = (p % BLOCK)[:, None], np.arange(BLOCK)[None, :]
    seen = (query // 16 == key // 16) & (key <= query)
    c[:, C_MASK:C_MASK + BLOCK] = np.where(seen, 0.0, -1e30)
    c[:, C_SLOT:C_SLOT + 4] = (p // D_HEAD % 4)[:, None] == np.arange(4)[None, :]
    c[:, C_DOMAIN:C_DOMAIN + 2] = (p[:, None] + 128 * np.arange(2)[None, :]) // EXPAND
    return c


def kernel(**inputs):
    import numpy as np
    import concourse.bacc as bacc
    from concourse.bass_utils import run_bass_kernel_spmd

    a = {k: np.asarray(v) for k, v in inputs.items()}
    order = a["x"].reshape(SEQ // DILATION, DILATION, BATCH).transpose(2, 1, 0).reshape(N_CHUNK, 2, 128)
    in_ctx_order = a["L0_attn_Wo"].T.reshape(4, 4, D_HEAD, DIM).transpose(1, 0, 2, 3).reshape(DIM, DIM)
    bv_in_ctx_order = a["L0_attn_bv"].reshape(4, 4, D_HEAD).transpose(1, 0, 2).reshape(DIM)
    wv_in_quad_order = a["L0_attn_Wv"].T.reshape(DIM, 4, 4, D_HEAD).transpose(0, 1, 3, 2).reshape(DIM, DIM)
    per_feature = [a["L0_attn_bq"], a["L0_attn_bk"], bv_in_ctx_order, np.repeat(a["L0_attn_beta"], D_HEAD)]
    arrays = {
        "ids": order.transpose(0, 2, 1).reshape(N_CHUNK * 128, 2),
        "domain_map": a["L0_tok_domain_map"].reshape(VOCAB, 1),
        "emb_table": a["L0_tok_emb_table"],
        "w_exp": a["L0_tok_W_exp"].reshape(DIM, DIM).T,
        "w_proj": a["L0_tok_W_proj"].transpose(0, 2, 1).reshape(DIM, DIM),
        "wq": a["L0_attn_Wq"].T, "wk": a["L0_attn_Wk"].T, "wv": wv_in_quad_order, "wo": in_ctx_order,
        "columns": np.stack([x.reshape(HALVES, 128).T for x in per_feature], 1),
        "bo": a["L0_attn_bo"],
        "wg": a["L0_ffn_Wg"], "bg": a["L0_ffn_bg"], "we": a["L0_ffn_We"], "be": a["L0_ffn_be"],
        "consts": lay_out_constants(),
    }
    arrays = {k: np.ascontiguousarray(v) for k, v in arrays.items()}
    nc = bacc.Bacc("TRN2", target_bir_lowering=False, num_devices=1)
    args = {k: nc.dram_tensor(k, v.shape, mybir.dt.from_np(v.dtype), kind="ExternalInput").ap()
            for k, v in arrays.items()}
    out = nc.dram_tensor("out", (TOKENS, DIM), FP32, kind="ExternalOutput").ap()
    build_lm_tower(nc, out=out, **args)
    r = run_bass_kernel_spmd(nc, [arrays], core_ids=[0])
    got = np.asarray(r.results[0]["out"])
    return got.reshape(BATCH, DILATION, SEQ // DILATION, DIM).transpose(2, 1, 0, 3).reshape(SEQ, BATCH, DIM)
```
